# Optimizing a Trainium2 kernel written in Bass

```python
import numpy as np
import jax
import jax.numpy as jnp

def _softmax(x, axis=-1):
    return jax.nn.softmax(x, axis=axis)

def _gelu(x):
    return jax.nn.gelu(x, approximate=True)

def _silu(x):
    return jax.nn.silu(x)

def _sigmoid(x):
    return jax.nn.sigmoid(x)

def _layernorm(x, axis=-1, eps=1e-05):
    m = jnp.mean(x, axis=axis, keepdims=True)
    v = jnp.var(x, axis=axis, keepdims=True)
    return (x - m) / jnp.sqrt(v + eps)

def _scatter_add(tgt, idx, src, axis=0):
    return tgt.at[idx].add(src)

def _segment_sum(src, seg, n):
    return jax.ops.segment_sum(src, seg, n)
kernel_name = 'mk_seq_postln_d1_jaxref_r4_b1f5cf'

def setup_inputs(seed: int=0):
    np.random.seed(seed)
    _w = jnp.asarray

    def _L0_attn_setup():
        import jax, jax.numpy as jnp
        import numpy as np
        B, SQ, HIDDEN = (2, 512, 512)
        HEADS, GROUPS, KVC = (16, 4, 128)
        HPG = HEADS // GROUPS
        LAYER_INDEX = 1
        SCALE = KVC ** (-0.5)
        key = jax.random.key(seed)
        k1, k2, k3, k4 = jax.random.split(key, 4)
        return {'x': jax.random.normal(k1, (B, SQ, HIDDEN), jnp.float32), 'w_q': jax.random.normal(k2, (HIDDEN, HEADS * KVC), jnp.float32) * 0.02, 'w_kv': jax.random.normal(k3, (HIDDEN, 2 * GROUPS * KVC), jnp.float32) * 0.02, 'w_dense': jax.random.normal(k4, (HEADS * KVC, HIDDEN), jnp.float32) * 0.02}
    _L0_attn_in = _L0_attn_setup()

    def _L0_ffn_setup():
        import jax, jax.numpy as jnp
        import numpy as np
        D_MODEL = 512
        D_EXPERT = 2048
        EPS = 1e-08

        def ternary_quant(w):
            scale = jnp.mean(jnp.abs(w)) + EPS
            q = jnp.clip(jnp.round(w / scale), -1.0, 1.0) * scale
            return w + jax.lax.stop_gradient(q - w)
        key = jax.random.key(seed)
        k_x, k_up, k_gate, k_down = jax.random.split(key, 4)
        std_in = 1.0 / np.sqrt(D_MODEL)
        std_exp = 1.0 / np.sqrt(D_EXPERT)
        return {'x': jax.random.normal(k_x, (4, 512, D_MODEL), dtype=jnp.float32), 'W_up': jax.random.normal(k_up, (D_EXPERT, D_MODEL), dtype=jnp.float32) * std_in, 'W_gate': jax.random.normal(k_gate, (D_EXPERT, D_MODEL), dtype=jnp.float32) * std_in, 'W_down': jax.random.normal(k_down, (D_MODEL, D_EXPERT), dtype=jnp.float32) * std_exp}
    _L0_ffn_in = _L0_ffn_setup()
    _d = {'L0_attn_x': _L0_attn_in['x'], 'L0_attn_w_q': _L0_attn_in['w_q'], 'L0_attn_w_kv': _L0_attn_in['w_kv'], 'L0_attn_w_dense': _L0_attn_in['w_dense'], 'L0_ffn_W_up': _L0_ffn_in['W_up'], 'L0_ffn_W_gate': _L0_ffn_in['W_gate'], 'L0_ffn_W_down': _L0_ffn_in['W_down']}
    _x0 = _d['L0_attn_x']
    _d['L0_attn_x'] = jax.random.normal(jax.random.fold_in(jax.random.key(seed), 1), (4, 512, 512), dtype=_x0.dtype)
    del _x0
    return _d

def reference(L0_attn_x, L0_attn_w_q, L0_attn_w_kv, L0_attn_w_dense, L0_ffn_W_up, L0_ffn_W_gate, L0_ffn_W_down):

    def _L0_attn_ref(x, w_q, w_kv, w_dense):
        import jax, jax.numpy as jnp
        import numpy as np
        B, SQ, HIDDEN = (2, 512, 512)
        HEADS, GROUPS, KVC = (16, 4, 128)
        HPG = HEADS // GROUPS
        LAYER_INDEX = 1
        SCALE = KVC ** (-0.5)
        b, sq, _ = x.shape
        sk = sq
        q = jnp.einsum('bsh,he->bse', x, w_q).reshape(b, sq, GROUPS, HPG, KVC)
        kv = jnp.einsum('bsh,he->bse', x, w_kv)
        k, v = jnp.split(kv, 2, axis=-1)
        k = k.reshape(b, sk, GROUPS, KVC)
        v = v.reshape(b, sk, GROUPS, KVC)
        scores = jnp.einsum('bqgpd,bkgd->bgqpk', q, k) * (SCALE / LAYER_INDEX)
        scores = scores.astype(jnp.float32) * LAYER_INDEX
        causal = jnp.arange(sq)[:, None] >= jnp.arange(sk)[None, :]
        scores = jnp.where(causal[None, None, :, None, :], scores, -jnp.inf)
        probs = jax.nn.softmax(scores, axis=-1).astype(x.dtype)
        ctx = jnp.einsum('bgqpk,bkgd->bqgpd', probs, v).reshape(b, sq, HEADS * KVC)
        return jnp.einsum('bse,eh->bsh', ctx, w_dense)

    def _L0_ffn_ref(x, W_up, W_gate, W_down):
        import jax, jax.numpy as jnp
        import numpy as np
        D_MODEL = 512
        D_EXPERT = 2048
        EPS = 1e-08

        def ternary_quant(w):
            scale = jnp.mean(jnp.abs(w)) + EPS
            q = jnp.clip(jnp.round(w / scale), -1.0, 1.0) * scale
            return w + jax.lax.stop_gradient(q - w)
        wu = ternary_quant(W_up)
        wg = ternary_quant(W_gate)
        wd = ternary_quant(W_down)
        up = jnp.einsum('bsd,ed->bse', x, wu)
        gate = jnp.einsum('bsd,ed->bse', x, wg)
        hidden = jax.nn.silu(up) * gate
        return jnp.einsum('bse,de->bsd', hidden, wd)
    x = L0_attn_x
    x = _layernorm(x + _L0_attn_ref(x, L0_attn_w_q, L0_attn_w_kv, L0_attn_w_dense), axis=-1)
    x = _layernorm(x + _L0_ffn_ref(x, L0_ffn_W_up, L0_ffn_W_gate, L0_ffn_W_down), axis=-1)
    return x

_drawn_inputs = setup_inputs


def setup_inputs(seed=0):
    import zlib

    import numpy as np

    out = dict(_drawn_inputs(seed))
    spreads = {}
    factors = {'L0_attn_w_q': 6.013}
    for name, (base, spread) in spreads.items():
        noise = np.random.default_rng([zlib.crc32(name.encode()), seed]).standard_normal(out[name].shape)
        drawn = base * np.exp(spread * noise) if base else spread * noise
        out[name] = jnp.asarray(drawn.astype(out[name].dtype))
    for name, factor in factors.items():
        out[name] = (out[name] * factor).astype(out[name].dtype)
    return out
```

```python
from contextlib import ExitStack

import concourse.bass as bass
from concourse import mybir

F32 = mybir.dt.float32
F32R = mybir.dt.float32r
ALU = mybir.AluOpType
ACT = mybir.ActivationFunctionType

P = 128
B = 4
S = 512
D = 512
KT = D // P
G = 4
HPG = 4
DH = 128
E = 2048
C = 4
ET = E // C // P
QT = S // P
N = B * HPG
SCALE = DH ** -0.5
LN_EPS = 1e-5
QUANT_EPS = 1e-8
NEG = -3.0e38

TILE_ORDER = (0, 2, 1, 3)
S_PSUM = {0: 0, 2: 128, 1: 512, 3: 1024}
S_SBUF = {0: 0, 2: 128, 1: 512, 3: 768}
PW = 1280
PT_AT = {0: 0, 1: 512, 3: 896, 2: 1024}
PT_CHUNKS = (((0,), 0, 512), ((1, 3), 512, 512), ((2,), 1024, 256))

RAW = 5
FRAW = 4


def layer(nc, x, x_t, w_q, w_k, w_v, w_dense, w_up, w_gate, w_down, out):
    with ExitStack() as ctx:
        def sb(name, shape, dt=F32):
            return ctx.enter_context(nc.sbuf_tensor(name, shape, dt))

        def sem(name):
            return ctx.enter_context(nc.semaphore(name))

        xt_hi = sb("xt_hi", [P, KT, B * S], F32R)
        xt_lo = sb("xt_lo", [P, KT, B * S], F32R)
        resid = sb("resid", [P, B * QT, D])
        wa_hi = sb("wa_hi", [P, HPG, KT * P], F32R)
        wa_lo = sb("wa_lo", [P, HPG, KT * P], F32R)
        wd_hi = sb("wd_hi", [P, HPG, D], F32R)
        wd_lo = sb("wd_lo", [P, HPG, D], F32R)
        wk_hi = sb("wk_hi", [P, KT * P], F32R)
        wk_lo = sb("wk_lo", [P, KT * P], F32R)
        wv_hi = sb("wv_hi", [P, KT * P], F32R)
        wv_lo = sb("wv_lo", [P, KT * P], F32R)
        raw = sb("raw", [P, RAW, 512])
        fraw = sb("fraw", [P, FRAW, 512])
        qt_hi = sb("qt_hi", [P, S], F32R)
        qt_lo = sb("qt_lo", [P, S], F32R)
        kt_hi = sb("kt_hi", [P, S], F32R)
        kt_lo = sb("kt_lo", [P, S], F32R)
        vt = sb("vt", [P, S])
        v_hi = sb("v_hi", [P, S], F32R)
        v_lo = sb("v_lo", [P, S], F32R)
        probs = sb("probs", [P, 2, PW])
        pt_hi = sb("pt_hi", [P, PW], F32R)
        pt_lo = sb("pt_lo", [P, PW], F32R)
        mid_hi = sb("mid_hi", [P, 2, HPG, S], F32R)
        mid_lo = sb("mid_lo", [P, 2, HPG, S], F32R)
        mask = sb("mask", [P, S], mybir.dt.bfloat16)
        ident = sb("ident", [P, P])
        ones = sb("ones", [P, P])
        rowmax = sb("rowmax", [P, 2, QT])
        negmax = sb("negmax", [P, 2, QT])
        rowsum = sb("rowsum", [P, 2, QT])
        rinv = sb("rinv", [P, 2, QT])
        abs_part = sb("abs_part", [P, 3, ET])
        abs_tot = sb("abs_tot", [P, 3, ET])
        abs_sum = sb("abs_sum", [P, 4])
        scales = sb("scales", [P, 4])
        thr = sb("thr", [P, 4])
        nthr = sb("nthr", [P, 4])
        stats = sb("stats", [P, QT, 6])
        mv = sb("mv", [P, QT, 2])
        std = sb("std", [P, QT])
        rstd = sb("rstd", [P, QT])
        eps = sb("eps", [P, 1])

        ps = ctx.enter_context(nc.psum_tensor("ps", [P, 8, 512], F32))
        flat = ps[:, :, :].rearrange("p a b -> p (a b)")
        PT_BANKS, Q_BANK, CTX_BANK, OUT_BANK = (3, 4, 3), 5, 6, 7
        UP_BANK, GATE_BANK, DOWN_BANK, LN_BANK = 0, 2, 4, 6

        sil = probs[:, 0, 0:1024].rearrange("p (a s) -> p a s", a=2)
        hid = probs[:, 1, 0:1024].rearrange("p (a s) -> p a s", a=2)
        tern_a = vt

        x_nat = x.rearrange("b (t p) d -> b p t d", p=P)
        out_nat = out.rearrange("b (t p) d -> b p t d", p=P)

        raw_landed = [sem(f"raw_landed{i}") for i in range(RAW)]
        fraw_landed = [sem(f"fraw_landed{i}") for i in range(FRAW)]
        resid_loaded = sem("resid_loaded")
        zeroed = sem("zeroed")
        consts = sem("consts")
        x_hi_done = sem("x_hi_done")
        x_split = sem("x_split")
        x_hi_pool = sem("x_hi_pool")
        x_split_pool = sem("x_split_pool")
        w_hi_done = sem("w_hi_done")
        wk_split = sem("wk_split")
        wq_split = sem("wq_split")
        wv_split = sem("wv_split")
        wd_split = sem("wd_split")
        w_split = sem("w_split")
        q_ready = sem("q_ready")
        k_ready = sem("k_ready")
        vt_ready = sem("vt_ready")
        v_ready = sem("v_ready")
        scores_ready = sem("scores_ready")
        pt_ready = sem("pt_ready")
        ctx_ready = sem("ctx_ready")
        out_ready = sem("out_ready")
        q_hi = sem("q_hi")
        k_hi = sem("k_hi")
        vt_copied = sem("vt_copied")
        v_hi_done = sem("v_hi_done")
        exp_done = sem("exp_done")
        pt_hi_done = sem("pt_hi_done")
        ctx_hi = sem("ctx_hi")
        abs_done = sem("abs_done")
        q_split = sem("q_split")
        k_split = sem("k_split")
        v_split = sem("v_split")
        masked = sem("masked")
        negmax_done = sem("negmax_done")
        rinv_done = sem("rinv_done")
        pt_split = sem("pt_split")
        ctx_split = sem("ctx_split")
        out_added = sem("out_added")
        abs_added = sem("abs_added")
        tot_done = sem("tot_done")
        step = sem("step")
        scales_done = sem("scales_done")
        pool_passed = sem("pool_passed")
        dve_passed = sem("dve_passed")
        normed = sem("normed")
        tot_ready = sem("tot_ready")
        stats_done = sem("stats_done")
        std_done = sem("std_done")
        ln_done = sem("ln_done")
        x1t_ready = sem("x1t_ready")
        x1t_hi = sem("x1t_hi")
        x1t_split = sem("x1t_split")
        tern_step = sem("tern_step")
        wu_tern = sem("wu_tern")
        wg_tern = sem("wg_tern")
        wdn_tern = sem("wdn_tern")
        tern_done = sem("tern_done")
        up_ready = sem("up_ready")
        gate_ready = sem("gate_ready")
        down_ready = sem("down_ready")
        silu_done = sem("silu_done")
        hid_done = sem("hid_done")
        hid_hi = sem("hid_hi")
        hid_split = sem("hid_split")
        down_added = sem("down_added")
        stored = sem("stored")

        first = ([("x", 0, 0), ("k", 0, 0), ("x", 0, 1), ("q", 0, 0), ("x", 0, 2), ("x", 0, 3), ("v", 0, 0)]
                 + [("q", 0, h) for h in (1, 2, 3)] + [("x", b, k) for b in (1, 2, 3) for k in range(KT)])
        current = [("d", 0, h) for h in range(HPG)]
        ahead = [("k", 1, 0), ("q", 1, 0), ("v", 1, 0), ("q", 1, 1), ("q", 1, 2), ("q", 1, 3)]
        PER_G = len(current) + len(ahead)
        assert PER_G % RAW == 0
        N_FIRST = len(first)
        slot_of = {}
        landed_at = {}
        for m, piece in enumerate(first):
            slot_of["first", piece] = m % RAW
            landed_at["first", piece] = 16 * (m // RAW + 1)
        for m, piece in enumerate(current + ahead):
            slot_of["loop", piece] = (N_FIRST + m) % RAW
            landed_at["loop", piece] = 16 * ((N_FIRST + m) // RAW + 1)
        PER_SLOT = 16 * (PER_G // RAW)
        on_vector = [p for p in first if p[0] == "x" and p[1] < 2]
        on_pool_x = [p for p in first if p[0] == "x" and p[1] >= 2]
        on_pool_w = [p for p in first if p[0] != "x"]
        NW_FIRST = len(on_pool_w)

        def source(piece, g):
            kind, ahead_by, j = piece
            if kind == "x":
                return x_t[ahead_by, j]
            at = g if ahead_by == 0 else nc.s_assert_within(g + 1, 1, G - 1, skip_runtime_bounds_check_because="the branch holds it below the last")
            return {"k": w_k, "v": w_v}[kind][at] if kind in "kv" else {"q": w_q, "d": w_dense}[kind][at, j]

        START = 5

        block = ctx.enter_context(nc.Block())

        @block.sync
        def _(sp):
            def release(piece):
                if piece in on_vector:
                    sp.wait_ge(x_split, on_vector.index(piece) + 1)
                elif piece in on_pool_x:
                    sp.wait_ge(x_split_pool, on_pool_x.index(piece) + 1)
                else:
                    sp.wait_ge(w_split, on_pool_w.index(piece) + 1)

            for m, piece in enumerate(first):
                if m >= RAW:
                    release(first[m - RAW])
                sp.dma_start(raw[:, m % RAW, :], source(piece, 0)).then_inc(raw_landed[m % RAW], 16)
                if m == 12:
                    for b in range(B):
                        sp.dma_start(resid[:, b * QT:(b + 1) * QT, :], x_nat[b]).then_inc(resid_loaded, 16)

            for piece in first[-RAW:]:
                release(piece)
            with sp.Fori(0, G) as g:
                def load(m):
                    piece = (current + ahead)[m]
                    s = slot_of["loop", piece]
                    if m >= RAW:
                        sp.wait_ge(w_split, g * PER_G + NW_FIRST + m - RAW + 1)
                    sp.dma_start(raw[:, s, :], source(piece, g)).then_inc(raw_landed[s], 16)

                def load_ffn(n):
                    which, et = divmod(n, ET)
                    s = n % FRAW
                    if n >= FRAW:
                        sp.wait_ge(abs_done, START + g * 3 * ET + n - FRAW + 1)
                    sp.dma_start(fraw[:, s, :], (w_up, w_gate, w_down)[which][g, et]).then_inc(fraw_landed[s], 16)

                sp.wait_ge(w_split, g * PER_G + NW_FIRST)
                sp.wait_ge(abs_done, START + g * 3 * ET)
                for m in range(4):
                    load(m)
                for n in range(3 * ET):
                    load_ffn(n)
                    with_next = {5: (4,), 6: (5,), 7: (6,), 8: (7,), 9: (8,)}
                    if n in with_next:
                        with sp.If(g < G - 1):
                            for m in with_next[n]:
                                load(m)
                with sp.If(g < G - 1):
                    load(9)

            sp.wait_ge(abs_done, START + G * 3 * ET)
            order0 = [(w, et) for et in range(ET) for w in (0, 1)]
            for m, (w, et) in enumerate(order0):
                if m >= FRAW:
                    sp.wait_ge(tern_done, m - FRAW + 1)
                sp.dma_start(fraw[:, m % FRAW, :], (w_up, w_gate)[w][0, et]).then_inc(fraw_landed[m % FRAW], 16)
            with sp.Fori(0, C) as c:
                for m in range(3 * ET):
                    if m < ET:
                        sp.wait_ge(tern_done, c * 3 * ET + 2 * ET + m - FRAW + 1)
                        sp.dma_start(fraw[:, m % FRAW, :], w_down[c, m]).then_inc(fraw_landed[m % FRAW], 16)
                with sp.If(c < C - 1):
                    for m, (w, et) in enumerate(order0):
                        m += ET
                        sp.wait_ge(tern_done, c * 3 * ET + 2 * ET + m - FRAW + 1)
                        sp.dma_start(fraw[:, m % FRAW, :], (w_up, w_gate)[w][nc.s_assert_within(c + 1, 1, C - 1, skip_runtime_bounds_check_because="the branch holds it below the last"), et]).then_inc(
                            fraw_landed[m % FRAW], 16)

            for b in range(B):
                sp.wait_ge(ln_done, B * QT + (b + 1) * QT)
                sp.dma_start(out_nat[b], resid[:, b * QT:(b + 1) * QT, :]).then_inc(stored, 16)
            sp.wait_ge(stored, 16 * B)

        @block.gpsimd
        def _(pool):
            pool.sem_inc(normed, START)
            nc.gpsimd.memset(mask[:], 0.0).then_inc(zeroed, 1)
            nc.gpsimd.memset(ident[:], 0.0).then_inc(zeroed, 1)
            nc.gpsimd.memset(ones[:], 1.0).then_inc(consts, 1)
            nc.gpsimd.memset(eps[:], LN_EPS).then_inc(consts, 1)
            nc.gpsimd.memset(abs_tot[:], 0.0).then_inc(consts, 1)
            pool.wait_ge(zeroed, 2)
            nc.gpsimd.affine_select(out=mask[:, S - P:S], in_=mask[:, S - P:S], compare_op=ALU.is_ge, fill=NEG,
                                    base=0, pattern=[[-1, P]], channel_multiplier=1).then_inc(consts, 1)
            nc.gpsimd.affine_select(out=ident[:], in_=ident[:], compare_op=ALU.not_equal, fill=1.0,
                                    base=0, pattern=[[-1, P]], channel_multiplier=1).then_inc(consts, 1)

            def wait_apart():
                pool.sem_inc(pool_passed, 1)

            def weight(piece, phase, base_landed, n_hi):
                kind, _, j = piece
                s = slot_of[phase, piece]
                pool.wait_ge(raw_landed[s], base_landed + landed_at[phase, piece])
                hi, lo, done = {"k": (wk_hi[:], wk_lo[:], wk_split), "v": (wv_hi[:], wv_lo[:], wv_split),
                                "q": (wa_hi[:, j, :], wa_lo[:, j, :], wq_split),
                                "d": (wd_hi[:, j, :], wd_lo[:, j, :], wd_split)}[kind]
                wait_apart()
                nc.gpsimd.tensor_copy(hi, raw[:, s, :]).then_inc(w_hi_done, 1)
                pool.wait_ge(w_hi_done, n_hi)
                nc.gpsimd.tensor_tensor(lo, raw[:, s, :], hi.bitcast(F32), ALU.subtract).then_inc(w_split, 1)
                pool.wait_ge(w_split, n_hi)
                pool.sem_inc(done, 1)

            for m, piece in enumerate(on_pool_w):
                weight(piece, "first", 0, m + 1)
            for m, piece in enumerate(on_pool_x):
                _, b, k = piece
                s = slot_of["first", piece]
                pool.wait_ge(raw_landed[s], landed_at["first", piece])
                hi, lo = xt_hi[:, k, b * S:(b + 1) * S], xt_lo[:, k, b * S:(b + 1) * S]
                nc.gpsimd.tensor_copy(hi, raw[:, s, :]).then_inc(x_hi_pool, 1)
                pool.wait_ge(x_hi_pool, m + 1)
                nc.gpsimd.tensor_tensor(lo, raw[:, s, :], hi.bitcast(F32), ALU.subtract).then_inc(x_split_pool, 1)

            with pool.Fori(0, G) as g:
                for n in range(N):
                    pool.wait_ge(rinv_done, g * N + n + 1)
                    wait_apart()
                    for i in TILE_ORDER:
                        t = probs[:, n % 2, S_SBUF[i]:S_SBUF[i] + P * (i + 1)]
                        nc.gpsimd.tensor_scalar(t, t, rinv[:, n % 2, i:i + 1], None, ALU.mult).then_inc(normed, 1)
                    if n in (2, 3):
                        pool.wait_ge(out_ready, START + g * N)
                        for m in (2 * (n - 2), 2 * (n - 2) + 1):
                            weight(current[m], "loop", g * PER_SLOT, g * PER_G + NW_FIRST + m + 1)
                    when = {12: (0, 1), 13: (2, 3), 14: (4,), 15: (5,)}
                    if n in when:
                        with pool.If(g < G - 1):
                            for m in when[n]:
                                kind, _, j = ahead[m]
                                if kind == "k":
                                    pool.wait_ge(k_ready, g * B + B)
                                elif kind == "v":
                                    pool.wait_ge(vt_ready, g * B + B)
                                else:
                                    pool.wait_ge(q_ready, g * N + N - HPG + j + 1)
                                weight(ahead[m], "loop", g * PER_SLOT, g * PER_G + NW_FIRST + 4 + m + 1)

            pool.wait_ge(scales_done, 1)
            LANDED0 = 16 * (G * 3 * ET // FRAW)

            def ternary(dst, which, m, base_landed, n_done, done):
                s = m % FRAW
                pool.wait_ge(fraw_landed[s], base_landed + LANDED0 + 16 * (m // FRAW + 1))
                src = fraw[:, s, :]
                wait_apart()
                nc.gpsimd.tensor_scalar(tern_a[:], src, nthr[:, which:which + 1], None, ALU.is_lt).then_inc(tern_step, 1)
                nc.gpsimd.tensor_scalar(src, src, thr[:, which:which + 1], None, ALU.is_gt).then_inc(tern_step, 1)
                pool.wait_ge(tern_step, 2 * n_done + 2)
                nc.gpsimd.tensor_tensor(dst, src, tern_a[:], ALU.subtract).then_inc(tern_done, 1)
                pool.wait_ge(tern_done, n_done + 1)
                pool.sem_inc(done, 1)

            pool.wait_ge(q_ready, G * N)
            pool.wait_ge(v_ready, G * B)
            for m in range(2 * ET):
                et, w = divmod(m, 2)
                ternary((wa_hi, wa_lo)[w][:, et, :], w, m, 0, m, (wu_tern, wg_tern)[w])
            pool.wait_ge(out_ready, START + G * N)
            with pool.Fori(0, C) as c:
                PER_C = 16 * (3 * ET // FRAW)
                pool.wait_ge(down_ready, START + c * N)
                for et in range(ET):
                    m = 2 * ET + et
                    ternary(wd_hi[:, et, :], 2, m, c * PER_C, c * 3 * ET + m, wdn_tern)
                with pool.If(c < C - 1):
                    for mm in range(2 * ET):
                        et, w = divmod(mm, 2)
                        m = 3 * ET + mm
                        pool.wait_ge((up_ready, gate_ready)[w], c * N + N - ET + et + 1)
                        ternary((wa_hi, wa_lo)[w][:, et, :], w, m, c * PER_C, c * 3 * ET + m, (wu_tern, wg_tern)[w])

        @block.scalar
        def _(act):
            copy = nc.scalar.copy
            for s in (pt_hi_done, ctx_hi, abs_done):
                act.sem_inc(s, START)
            for m, piece in enumerate(on_vector):
                _, b, k = piece
                s = slot_of["first", piece]
                act.wait_ge(raw_landed[s], landed_at["first", piece])
                copy(xt_hi[:, k, b * S:(b + 1) * S], raw[:, s, :]).then_inc(x_hi_done, 1)
                if m == KT - 1:
                    act.wait_ge(k_ready, 1)
                    copy(kt_hi[:], ps[:, OUT_BANK, :]).then_inc(k_hi, 1)
                    act.wait_ge(q_ready, 1)
                    copy(qt_hi[:], ps[:, Q_BANK, :]).then_inc(q_hi, 1)

            def pt_evacuate(head, chunk):
                _, at, w = PT_CHUNKS[chunk]
                act.wait_ge(pt_ready, START + head * 3 - 2 + chunk)
                copy(pt_hi[:, at:at + w], ps[:, PT_BANKS[chunk], 0:w]).then_inc(pt_hi_done, 1)

            def ctx_evacuate(head, b, h):
                act.wait_ge(ctx_ready, START + head)
                copy(mid_hi[:, b % 2, h, :], ps[:, CTX_BANK, :]).then_inc(ctx_hi, 1)

            def next_q(g, n):
                act.wait_ge(q_ready, g * N + n + 2)
                copy(qt_hi[:], ps[:, Q_BANK, :]).then_inc(q_hi, 1)

            def next_k(g, b):
                act.wait_ge(k_ready, g * B + b + 2)
                copy(kt_hi[:], ps[:, OUT_BANK, :]).then_inc(k_hi, 1)

            with act.Fori(0, G) as g:
                for n in range(N):
                    b, h = divmod(n, HPG)
                    before = (b, h - 1) if h else ((b - 1) % B, HPG - 1)
                    if n:
                        pt_evacuate(g * N + n, 0)
                        pt_evacuate(g * N + n, 1)
                    else:
                        with act.If(g > 0):
                            pt_evacuate(g * N + n, 0)
                            pt_evacuate(g * N + n, 1)
                    act.wait_ge(negmax_done, g * N + n + 1)
                    for i in TILE_ORDER:
                        t = probs[:, n % 2, S_SBUF[i]:S_SBUF[i] + P * (i + 1)]
                        nc.scalar.activation(t, t, ACT.Exp, bias=negmax[:, n % 2, i:i + 1], scale=SCALE,
                                             accum_out=rowsum[:, n % 2, i:i + 1]).then_inc(exp_done, 1)
                    if n < N - 1:
                        next_q(g, n)
                    else:
                        with act.If(g < G - 1):
                            next_q(g, n)
                    if n:
                        pt_evacuate(g * N + n, 2)
                    else:
                        with act.If(g > 0):
                            pt_evacuate(g * N + n, 2)
                    if h == 3:
                        if b < B - 1:
                            next_k(g, b)
                        else:
                            with act.If(g < G - 1):
                                next_k(g, b)
                    if h == 0:
                        act.wait_ge(vt_ready, g * B + b + 1)
                        copy(vt[:], ps[:, OUT_BANK, :]).then_inc(vt_copied, 1)
                    if n:
                        ctx_evacuate(g * N + n, *before)
                    else:
                        with act.If(g > 0):
                            ctx_evacuate(g * N + n, *before)
                    if h == 0:
                        act.wait_ge(v_ready, g * B + b + 1)
                        copy(v_hi[:], ps[:, OUT_BANK, :]).then_inc(v_hi_done, 1)
                    if n < 3 * ET:
                        which, et = divmod(n, ET)
                        s = n % FRAW
                        act.wait_ge(fraw_landed[s], g * 16 * (3 * ET // FRAW) + 16 * (n // FRAW + 1))
                        act.wait_ge(abs_added, START + g)
                        nc.scalar.activation(fraw[:, s, :], fraw[:, s, :], ACT.Abs,
                                             accum_out=abs_part[:, which, et:et + 1]).then_inc(abs_done, 1)
            for chunk in range(3):
                pt_evacuate(G * N, chunk)
            ctx_evacuate(G * N, B - 1, HPG - 1)

            def layer_norm_std(batches):
                act.wait_ge(stats_done, batches)
                nc.scalar.activation(std[:], mv[:, :, 1], ACT.Sqrt, bias=eps[:, 0:1]).then_inc(std_done, 1)

            for b in range(B):
                layer_norm_std(b + 1)
                for k in range(KT):
                    act.wait_ge(x1t_ready, b * KT + k + 1)
                    copy(xt_hi[:, k, b * S:(b + 1) * S], ps[:, LN_BANK + k % 2, :]).then_inc(x1t_hi, 1)

            with act.Fori(0, C) as c:
                for u in range(N):
                    b, et = divmod(u, ET)
                    act.wait_ge(up_ready, c * N + u + 1)
                    if u >= 2:
                        act.wait_ge(hid_done, START + c * N + u - 1)
                    nc.scalar.activation(sil[:, u % 2, :], ps[:, UP_BANK + u % 2, :], ACT.Silu,
                                         scale=scales[:, 0:1]).then_inc(silu_done, 1)
                    act.wait_ge(hid_done, START + c * N + u + 1)
                    copy(mid_hi[:, b % 2, et, :], hid[:, u % 2, :]).then_inc(hid_hi, 1)
            for b in range(B):
                layer_norm_std(B + b + 1)

        @block.vector
        def _(dve):
            for s in (pt_split, ctx_split, out_added, down_added, masked, v_split, abs_added, hid_done, hid_split):
                dve.sem_inc(s, START)
            links = [0]

            def link(ins):
                links[0] += 1
                ins.then_inc(step, 1)
                dve.wait_ge(step, links[0])

            def low(lo, src, hi):
                return nc.vector.tensor_tensor(lo, src, hi.bitcast(F32), ALU.subtract)

            for m, piece in enumerate(on_vector):
                _, b, k = piece
                s = slot_of["first", piece]
                dve.wait_ge(x_hi_done, m + 1)
                low(xt_lo[:, k, b * S:(b + 1) * S], raw[:, s, :], xt_hi[:, k, b * S:(b + 1) * S]).then_inc(x_split, 1)
                if m == KT - 1:
                    dve.wait_ge(k_hi, 1)
                    low(kt_lo[:], ps[:, OUT_BANK, :], kt_hi[:]).then_inc(k_split, 1)
                    dve.wait_ge(q_hi, 1)
                    low(qt_lo[:], ps[:, Q_BANK, :], qt_hi[:]).then_inc(q_split, 1)
            dve.wait_ge(consts, 5)
            dve.wait_ge(resid_loaded, 16 * B)

            def pt_low(head, chunk):
                _, at, w = PT_CHUNKS[chunk]
                dve.wait_ge(pt_hi_done, START + head * 3 - 2 + chunk)
                low(pt_lo[:, at:at + w], ps[:, PT_BANKS[chunk], 0:w], pt_hi[:, at:at + w]).then_inc(pt_split, 1)

            def ctx_low(head, b, h):
                dve.wait_ge(ctx_hi, START + head)
                low(mid_lo[:, b % 2, h, :], ps[:, CTX_BANK, :], mid_hi[:, b % 2, h, :]).then_inc(ctx_split, 1)

            def next_q(g, n):
                dve.wait_ge(q_hi, g * N + n + 2)
                low(qt_lo[:], ps[:, Q_BANK, :], qt_hi[:]).then_inc(q_split, 1)

            def next_k(g, b):
                dve.wait_ge(k_hi, g * B + b + 2)
                low(kt_lo[:], ps[:, OUT_BANK, :], kt_hi[:]).then_inc(k_split, 1)

            def add_out(tiles, b, t):
                dve.wait_ge(out_ready, START + tiles)
                r = resid[:, b * QT + t, :]
                nc.vector.tensor_tensor(r, ps[:, OUT_BANK, :], r, ALU.add).then_inc(out_added, 1)

            with dve.Fori(0, G) as g:
                for n in range(N):
                    b, h = divmod(n, HPG)
                    before = (b, h - 1) if h else ((b - 1) % B, HPG - 1)
                    if n:
                        pt_low(g * N + n, 0)
                        pt_low(g * N + n, 1)
                    else:
                        with dve.If(g > 0):
                            pt_low(g * N + n, 0)
                            pt_low(g * N + n, 1)
                    for a, i in enumerate(TILE_ORDER):
                        w = P * (i + 1)
                        if a != 1:
                            dve.wait_ge(scores_ready, (g * N + n) * 3 + max(a, 1))
                            dve.sem_inc(dve_passed, 1)
                        nc.vector.tensor_tensor_reduce(
                            out=probs[:, n % 2, S_SBUF[i]:S_SBUF[i] + w], in0=flat[:, S_PSUM[i]:S_PSUM[i] + w],
                            in1=mask[:, S - w:S], scale=1.0, scalar=NEG, op0=ALU.add, op1=ALU.max,
                            accum_out=rowmax[:, n % 2, i:i + 1]).then_inc(masked, 1)
                    dve.wait_ge(masked, START + (g * N + n) * 4 + 4)
                    nc.vector.tensor_scalar(negmax[:, n % 2, :], rowmax[:, n % 2, :], -SCALE, None,
                                            ALU.mult).then_inc(negmax_done, 1)
                    tiles = {1: (0, 1), 2: (2, 3)}.get(h)
                    if tiles:
                        if b:
                            add_out(g * N + (b - 1) * QT + tiles[0] + 1, b - 1, tiles[0])
                        else:
                            with dve.If(g > 0):
                                add_out(g * N - QT + tiles[0] + 1, B - 1, tiles[0])
                    if n < N - 1:
                        next_q(g, n)
                    else:
                        with dve.If(g < G - 1):
                            next_q(g, n)
                    if n:
                        pt_low(g * N + n, 2)
                    else:
                        with dve.If(g > 0):
                            pt_low(g * N + n, 2)
                    dve.wait_ge(exp_done, (g * N + n) * 4 + 4)
                    nc.vector.reciprocal(rinv[:, n % 2, :], rowsum[:, n % 2, :]).then_inc(rinv_done, 1)
                    if tiles:
                        if b:
                            add_out(g * N + (b - 1) * QT + tiles[1] + 1, b - 1, tiles[1])
                        else:
                            with dve.If(g > 0):
                                add_out(g * N - QT + tiles[1] + 1, B - 1, tiles[1])
                    if h == 3:
                        if b < B - 1:
                            next_k(g, b)
                        else:
                            with dve.If(g < G - 1):
                                next_k(g, b)
                    if n:
                        ctx_low(g * N + n, *before)
                    else:
                        with dve.If(g > 0):
                            ctx_low(g * N + n, *before)
                    if h == 0:
                        dve.wait_ge(v_hi_done, g * B + b + 1)
                        low(v_lo[:], ps[:, OUT_BANK, :], v_hi[:]).then_inc(v_split, 1)
                dve.wait_ge(abs_done, START + (g + 1) * 3 * ET)
                dve.wait_ge(abs_added, START + g)
                nc.vector.tensor_tensor(abs_tot[:], abs_tot[:], abs_part[:], ALU.add).then_inc(abs_added, 1)

            dve.wait_ge(abs_added, START + G)
            nc.vector.tensor_reduce(abs_sum[:, 0:3], abs_tot[:], mybir.AxisListType.X, ALU.add).then_inc(tot_done, 1)
            dve.wait_ge(tot_ready, 1)
            link(nc.vector.tensor_scalar(scales[:, 0:3], ps[:, UP_BANK, 0:3], 1.0 / (D * E), QUANT_EPS, ALU.mult, ALU.add))
            link(nc.vector.tensor_scalar(thr[:, 0:3], scales[:, 0:3], 0.5, None, ALU.mult))
            link(nc.vector.tensor_scalar(nthr[:, 0:3], scales[:, 0:3], -0.5, None, ALU.mult))
            link(nc.vector.tensor_tensor(scales[:, 3:4], scales[:, 1:2], scales[:, 2:3], ALU.mult))
            dve.sem_inc(scales_done, 1)

            for chunk in range(3):
                pt_low(G * N, chunk)
            ctx_low(G * N, B - 1, HPG - 1)
            for t in range(QT):
                add_out(G * N - QT + t + 1, B - 1, t)

            def layer_norm(b, done, added=None):
                for t in range(QT):
                    nc.vector.bn_stats(stats[:, t, :], resid[:, b * QT + t, :]).then_inc(step, 1)
                links[0] += QT
                dve.wait_ge(step, links[0])
                for t in range(QT):
                    ins = nc.vector.bn_aggr(mv[:, t, :], stats[:, t, :]).then_inc(step, 1)
                links[0] += QT
                dve.wait_ge(step, links[0])
                dve.sem_inc(stats_done, 1)
                dve.wait_ge(std_done, done + 1)
                link(nc.vector.reciprocal(rstd[:], std[:]))
                for t in range(QT):
                    r = resid[:, b * QT + t, :]
                    nc.vector.tensor_scalar(r, r, mv[:, t, 0:1], rstd[:, t:t + 1], ALU.subtract,
                                            ALU.mult).then_inc(ln_done, 1)

            dve.wait_ge(out_added, START + G * N)
            for b in range(B):
                layer_norm(b, b)
                for k in range(KT):
                    dve.wait_ge(x1t_hi, b * KT + k + 1)
                    low(xt_lo[:, k, b * S:(b + 1) * S], ps[:, LN_BANK + k % 2, :],
                        xt_hi[:, k, b * S:(b + 1) * S]).then_inc(x1t_split, 1)

            def add_down(tiles, b, t):
                dve.wait_ge(down_ready, START + tiles)
                r = resid[:, b * QT + t, :]
                nc.vector.scalar_tensor_tensor(r, ps[:, DOWN_BANK + t % 2, :], scales[:, 3:4], r,
                                               ALU.mult, ALU.add).then_inc(down_added, 1)

            with dve.Fori(0, C) as c:
                for u in range(N):
                    b, et = divmod(u, ET)
                    dve.wait_ge(silu_done, c * N + u + 1)
                    dve.wait_ge(gate_ready, c * N + u + 1)
                    if u >= 2:
                        dve.wait_ge(hid_split, START + c * N + u - 1)
                    nc.vector.tensor_tensor(hid[:, u % 2, :], ps[:, GATE_BANK + u % 2, :], sil[:, u % 2, :],
                                            ALU.mult).then_inc(hid_done, 1)
                    tiles = {1: (0, 1), 2: (2, 3)}.get(et, ())
                    for t in tiles:
                        if b:
                            add_down(c * N + (b - 1) * QT + t + 1, b - 1, t)
                        else:
                            with dve.If(c > 0):
                                add_down(c * N - QT + t + 1, B - 1, t)
                    dve.wait_ge(hid_hi, c * N + u + 1)
                    low(mid_lo[:, b % 2, et, :], hid[:, u % 2, :], mid_hi[:, b % 2, et, :]).then_inc(hid_split, 1)
            for t in range(QT):
                add_down(C * N - QT + t + 1, B - 1, t)
            dve.wait_ge(down_added, START + C * N)
            for b in range(B):
                layer_norm(b, B + b)

        @block.tensor
        def _(pe):
            mm = nc.tensor.matmul
            for s in (pt_ready, out_ready, down_ready, ctx_ready):
                pe.sem_inc(s, START)

            def product(bank_ap, terms):
                for n, (w, v) in enumerate(terms):
                    last = mm(bank_ap, w, v, start=n == 0, stop=n == len(terms) - 1)
                return last

            def project(bank, w_hi, w_lo, b):
                at = slice(b * S, (b + 1) * S)
                return product(ps[:, bank, :], [
                    t for k in range(KT) for t in (
                        (w_hi[:, k * P:(k + 1) * P], xt_hi[:, k, at]),
                        (w_hi[:, k * P:(k + 1) * P], xt_lo[:, k, at]),
                        (w_lo[:, k * P:(k + 1) * P], xt_hi[:, k, at]))])

            def x_of(b):
                if b < 2:
                    pe.wait_ge(x_split, (b + 1) * KT)
                else:
                    pe.wait_ge(x_split_pool, (b - 1) * KT)

            def q_project(b, h):
                project(Q_BANK, wa_hi[:, h, :], wa_lo[:, h, :], b).then_inc(q_ready, 1)

            def k_project(b):
                project(OUT_BANK, wk_hi[:], wk_lo[:], b).then_inc(k_ready, 1)

            def transpose_chunk(par, chunk):
                js, _, _ = PT_CHUNKS[chunk]
                at = 0
                for j in js:
                    for i in range(j, QT):
                        last = nc.tensor.transpose(ps[:, PT_BANKS[chunk], at:at + P],
                                                   probs[:, par, S_SBUF[i] + j * P:S_SBUF[i] + (j + 1) * P], ident[:])
                        at += P
                last.then_inc(pt_ready, 1)

            def transposes_ab(heads, par):
                pe.wait_ge(normed, START + heads * 4 + 4)
                pe.wait_ge(pt_split, START + heads * 3)
                transpose_chunk(par, 0)
                transpose_chunk(par, 1)

            def transposes_c(heads, par):
                pe.wait_ge(pt_split, START + heads * 3 + 1)
                transpose_chunk(par, 2)

            def pv(heads, batches):
                pe.wait_ge(pt_split, START + heads * 3 + 3)
                pe.wait_ge(v_split, START + batches)
                pe.wait_ge(ctx_split, START + heads)
                n = 0
                for j in (0, 1, 3, 2):
                    w = S - j * P
                    at = PT_AT[j]
                    for v, p in ((v_hi, pt_hi), (v_hi, pt_lo), (v_lo, pt_hi)):
                        last = mm(ps[:, CTX_BANK, j * P:S], v[:, j * P:(j + 1) * P], p[:, at:at + w],
                                  start=n == 0, stop=n == 3 * QT - 1)
                        n += 1
                last.then_inc(ctx_ready, 1)

            def out_tile(tiles, par, t):
                pe.wait_ge(out_added, START + tiles)
                at = slice(t * P, (t + 1) * P)
                product(ps[:, OUT_BANK, :], [
                    t for h in range(HPG) for t in (
                        (mid_hi[:, par, h, at], wd_hi[:, h, :]),
                        (mid_hi[:, par, h, at], wd_lo[:, h, :]),
                        (mid_lo[:, par, h, at], wd_hi[:, h, :]))]).then_inc(out_ready, 1)

            x_of(0)
            pe.wait_ge(wk_split, 1)
            k_project(0)
            pe.wait_ge(wq_split, 1)
            q_project(0, 0)
            pe.wait_ge(consts, 5)

            with pe.Fori(0, G) as g:
                for n in range(N):
                    b, h = divmod(n, HPG)
                    if n:
                        transposes_ab(g * N + n - 1, (n - 1) % 2)
                    else:
                        with pe.If(g > 0):
                            transposes_ab(g * N + n - 1, (n - 1) % 2)

                    pe.wait_ge(q_split, g * N + n + 1)
                    if h == 0:
                        pe.wait_ge(k_split, g * B + b + 1)
                    pe.wait_ge(masked, START + (g * N + n) * 4)
                    for i in TILE_ORDER:
                        at, w = slice(i * P, (i + 1) * P), P * (i + 1)
                        last = product(flat[:, S_PSUM[i]:S_PSUM[i] + w], [
                            (qt_hi[:, at], kt_hi[:, 0:w]), (qt_hi[:, at], kt_lo[:, 0:w]), (qt_lo[:, at], kt_hi[:, 0:w])])
                        if i:
                            last.then_inc(scores_ready, 1)

                    tiles = {1: (0, 1), 2: (2, 3)}.get(h)

                    def out_of_batch_before(t, first):
                        if b:
                            if first:
                                pe.wait_ge(ctx_split, START + g * N + b * HPG)
                                pe.wait_ge(v_split, START + g * B + b + 1)
                                if b == 1:
                                    pe.wait_ge(wd_split, (g + 1) * HPG)
                            out_tile(g * N + (b - 1) * QT + t, (b - 1) % 2, t)
                        else:
                            with pe.If(g > 0):
                                if first:
                                    pe.wait_ge(ctx_split, START + g * N)
                                    pe.wait_ge(v_split, START + g * B + b + 1)
                                out_tile(g * N - QT + t, (B - 1) % 2, t)

                    if tiles:
                        out_of_batch_before(tiles[0], h == 1)

                    def next_q():
                        nb, nh = divmod((n + 1) % N, HPG)
                        if nh == 0:
                            x_of(nb)
                        if nb == 0:
                            pe.wait_ge(wq_split, (g + (1 if n == N - 1 else 0)) * HPG + nh + 1)
                        q_project(nb, nh)
                    if n < N - 1:
                        next_q()
                    else:
                        with pe.If(g < G - 1):
                            next_q()

                    if n:
                        transposes_c(g * N + n - 1, (n - 1) % 2)
                    else:
                        with pe.If(g > 0):
                            transposes_c(g * N + n - 1, (n - 1) % 2)

                    if tiles:
                        out_of_batch_before(tiles[1], False)
                    if h == 3:
                        if b < B - 1:
                            pe.wait_ge(out_added, START + g * N + b * QT)
                            k_project(b + 1)
                        else:
                            with pe.If(g < G - 1):
                                pe.wait_ge(out_added, START + g * N + b * QT)
                                pe.wait_ge(wk_split, g + 2)
                                k_project(0)
                    if h == 0:
                        if b == 0:
                            pe.wait_ge(wv_split, g + 1)
                        project(OUT_BANK, wv_hi[:], wv_lo[:], b).then_inc(vt_ready, 1)

                    def pv_before():
                        pv(g * N + n - 1, g * B + (b if h else b - 1) + 1)
                    if n:
                        pv_before()
                    else:
                        with pe.If(g > 0):
                            pv(g * N - 1, g * B)
                    if h == 0:
                        pe.wait_ge(vt_copied, g * B + b + 1)
                        for t in range(QT):
                            last = nc.tensor.transpose(ps[:, OUT_BANK, t * P:(t + 1) * P], vt[:, t * P:(t + 1) * P], ident[:])
                        last.then_inc(v_ready, 1)

            transposes_ab(G * N - 1, (N - 1) % 2)
            pe.wait_ge(tot_done, 1)
            mm(ps[:, UP_BANK, 0:3], ones[:], abs_sum[:, 0:3], start=True, stop=True).then_inc(tot_ready, 1)
            transposes_c(G * N - 1, (N - 1) % 2)
            pv(G * N - 1, G * B)
            pe.wait_ge(ctx_split, START + G * N)
            for t in range(QT):
                out_tile(G * N - QT + t, (B - 1) % 2, t)

            for b in range(B):
                pe.wait_ge(ln_done, (b + 1) * QT)
                for k in range(KT):
                    if b * KT + k >= 2:
                        pe.wait_ge(x1t_split, b * KT + k - 1)
                    else:
                        pe.wait_ge(out_added, START + G * N)
                    for t in range(QT):
                        last = nc.tensor.transpose(ps[:, LN_BANK + k % 2, t * P:(t + 1) * P],
                                                   resid[:, b * QT + t, k * P:(k + 1) * P], ident[:])
                    last.then_inc(x1t_ready, 1)

            def half(bank, w, b):
                at = slice(b * S, (b + 1) * S)
                return product(ps[:, bank, :], [
                    (w[:, k * P:(k + 1) * P], v[:, k, at]) for k in range(KT) for v in (xt_hi, xt_lo)])

            def down_tile(tiles, par, t):
                if t < 2:
                    pe.wait_ge(down_added, START + tiles - t)
                else:
                    pe.wait_ge(down_added, START + tiles - 1)
                at = slice(t * P, (t + 1) * P)
                product(ps[:, DOWN_BANK + t % 2, :], [
                    (v[:, par, et, at], wd_hi[:, et, :]) for et in range(ET) for v in (mid_hi, mid_lo)
                ]).then_inc(down_ready, 1)

            with pe.Fori(0, C) as c:
                for u in range(N):
                    b, et = divmod(u, ET)
                    if et == 0:
                        pe.wait_ge(x1t_split, (b + 1) * KT)
                    if u >= 2:
                        pe.wait_ge(hid_done, START + c * N + u - 1)
                    else:
                        pe.wait_ge(hid_done, START + c * N)
                    if b == 0:
                        pe.wait_ge(wu_tern, c * ET + et + 1)
                    half(UP_BANK + u % 2, wa_hi[:, et, :], b).then_inc(up_ready, 1)
                    if b == 0:
                        pe.wait_ge(wg_tern, c * ET + et + 1)
                    half(GATE_BANK + u % 2, wa_lo[:, et, :], b).then_inc(gate_ready, 1)
                    for t in {1: (0, 1), 2: (2, 3)}.get(et, ()):
                        if b:
                            if t == 0:
                                pe.wait_ge(hid_split, START + c * N + b * ET)
                                if b == 1:
                                    pe.wait_ge(wdn_tern, (c + 1) * ET)
                            down_tile(c * N + (b - 1) * QT + t, (b - 1) % 2, t)
                        else:
                            with pe.If(c > 0):
                                if t == 0:
                                    pe.wait_ge(hid_split, START + c * N)
                                down_tile(c * N - QT + t, (B - 1) % 2, t)
            pe.wait_ge(hid_split, START + C * N)
            for t in range(QT):
                down_tile(C * N - QT + t, (B - 1) % 2, t)


def kernel(**inputs):
    import numpy as np
    import concourse.bacc as bacc
    from concourse.bass_utils import run_bass_kernel_spmd as run

    x = np.ascontiguousarray(inputs["L0_attn_x"])
    w_kv = inputs["L0_attn_w_kv"]

    def by_column(w, n):
        return np.ascontiguousarray(np.asarray(w).reshape(KT, P, n, P).transpose(2, 1, 0, 3).reshape(n, P, KT * P))

    arrays = {
        "x": x,
        "x_t": np.ascontiguousarray(np.asarray(x).transpose(0, 2, 1).reshape(B, KT, P, S)),
        "w_q": by_column(inputs["L0_attn_w_q"], G * HPG).reshape(G, HPG, P, KT * P),
        "w_k": by_column(w_kv[:, :G * DH], G),
        "w_v": by_column(w_kv[:, G * DH:], G),
        "w_dense": np.ascontiguousarray(inputs["L0_attn_w_dense"]).reshape(G, HPG, P, D),
        "w_up": by_column(np.asarray(inputs["L0_ffn_W_up"]).T, C * ET).reshape(C, ET, P, KT * P),
        "w_gate": by_column(np.asarray(inputs["L0_ffn_W_gate"]).T, C * ET).reshape(C, ET, P, KT * P),
        "w_down": np.ascontiguousarray(np.asarray(inputs["L0_ffn_W_down"]).T).reshape(C, ET, P, D),
    }
    nc = bacc.Bacc("TRN2", target_bir_lowering=False, num_devices=1, dynamic_dma_scratch_size=1024)
    args = [nc.dram_tensor(f"in_{name}", a.shape, mybir.dt.from_np(a.dtype), kind="ExternalInput").ap()
            for name, a in arrays.items()]
    args.append(nc.dram_tensor("out", (B, S, D), F32, kind="ExternalOutput").ap())
    layer(nc, *args)
    r = run(nc, [{f"in_{name}": a for name, a in arrays.items()}], core_ids=[0])
    return r.results[0]["out"]
```

```python
from contextlib import ExitStack

import concourse.bass as bass
from concourse import mybir

F32 = mybir.dt.float32
F32R = mybir.dt.float32r
ALU = mybir.AluOpType
ACT = mybir.ActivationFunctionType

P = 128
B = 4
S = 512
D = 512
KT = D // P
G = 4
HPG = 4
DH = 128
E = 2048
C = 4
ET = E // C // P
QT = S // P
N = B * HPG
SCALE = DH ** -0.5
LN_EPS = 1e-5
QUANT_EPS = 1e-8
NEG = -3.0e38

TILE_ORDER = (0, 2, 1, 3)
S_PSUM = {0: 0, 2: 128, 1: 512, 3: 1024}
S_SBUF = {0: 0, 2: 128, 1: 512, 3: 768}
PW = 1280
PT_AT = {0: 0, 1: 512, 3: 896, 2: 1024}
PT_CHUNKS = (((0,), 0, 512), ((1, 3), 512, 512), ((2,), 1024, 256))

RAW = 5
FRAW = 4


def layer(nc, x, x_t, w_q, w_k, w_v, w_dense, w_up, w_gate, w_down, out):
    with ExitStack() as ctx:
        def sb(name, shape, dt=F32):
            return ctx.enter_context(nc.sbuf_tensor(name, shape, dt))

        def sem(name):
            return ctx.enter_context(nc.semaphore(name))

        xt_hi = sb("xt_hi", [P, KT, B * S], F32R)
        xt_lo = sb("xt_lo", [P, KT, B * S], F32R)
        resid = sb("resid", [P, B * QT, D])
        wa_hi = sb("wa_hi", [P, HPG, KT * P], F32R)
        wa_lo = sb("wa_lo", [P, HPG, KT * P], F32R)
        wd_hi = sb("wd_hi", [P, HPG, D], F32R)
        wd_lo = sb("wd_lo", [P, HPG, D], F32R)
        wk_hi = sb("wk_hi", [P, KT * P], F32R)
        wk_lo = sb("wk_lo", [P, KT * P], F32R)
        wv_hi = sb("wv_hi", [P, KT * P], F32R)
        wv_lo = sb("wv_lo", [P, KT * P], F32R)
        raw = sb("raw", [P, RAW, 512])
        fraw = sb("fraw", [P, FRAW, 512])
        qt_hi = sb("qt_hi", [P, S], F32R)
        qt_lo = sb("qt_lo", [P, S], F32R)
        kt_hi = sb("kt_hi", [P, S], F32R)
        kt_lo = sb("kt_lo", [P, S], F32R)
        vt = sb("vt", [P, S])
        v_hi = sb("v_hi", [P, S], F32R)
        v_lo = sb("v_lo", [P, S], F32R)
        probs = sb("probs", [P, 2, PW])
        pt_hi = sb("pt_hi", [P, PW], F32R)
        pt_lo = sb("pt_lo", [P, PW], F32R)
        mid_hi = sb("mid_hi", [P, 2, HPG, S], F32R)
        mid_lo = sb("mid_lo", [P, 2, HPG, S], F32R)
        mask = sb("mask", [P, S], mybir.dt.bfloat16)
        ident = sb("ident", [P, P])
        ones = sb("ones", [P, P])
        rowmax = sb("rowmax", [P, 2, QT])
        negmax = sb("negmax", [P, 2, QT])
        rowsum = sb("rowsum", [P, 2, QT])
        rinv = sb("rinv", [P, 2, QT])
        abs_part = sb("abs_part", [P, 3, ET])
        abs_tot = sb("abs_tot", [P, 3, ET])
        abs_sum = sb("abs_sum", [P, 4])
        scales = sb("scales", [P, 4])
        thr = sb("thr", [P, 4])
        nthr = sb("nthr", [P, 4])
        stats = sb("stats", [P, QT, 6])
        mv = sb("mv", [P, QT, 2])
        std = sb("std", [P, QT])
        rstd = sb("rstd", [P, QT])
        power = sb("power", [P, QT])

        ps = ctx.enter_context(nc.psum_tensor("ps", [P, 8, 512], F32))
        flat = ps[:, :, :].rearrange("p a b -> p (a b)")
        PT_BANKS, Q_BANK, CTX_BANK, OUT_BANK = (3, 4, 3), 5, 6, 7
        UP_BANK, GATE_BANK, DOWN_BANK, LN_BANK = 0, 2, 6, 4

        sil = probs[:, 0, 0:1024].rearrange("p (a s) -> p a s", a=2)
        hid = probs[:, 1, 0:1024].rearrange("p (a s) -> p a s", a=2)

        x_nat = x.rearrange("b (t p) d -> b p t d", p=P)
        out_nat = out.rearrange("b (t p) d -> b p t d", p=P)

        raw_landed = [sem(f"raw_landed{i}") for i in range(RAW)]
        fraw_landed = [sem(f"fraw_landed{i}") for i in range(FRAW)]
        resid_loaded = sem("resid_loaded")
        zeroed = sem("zeroed")
        consts = sem("consts")
        first_hi = sem("first_hi")
        first_split = sem("first_split")
        x_hi_pool = sem("x_hi_pool")
        x_split_pool = sem("x_split_pool")
        w_hi_done = sem("w_hi_done")
        wk_split = sem("wk_split")
        wq_split = sem("wq_split")
        wv_split = sem("wv_split")
        wd_split = sem("wd_split")
        w_split = sem("w_split")
        q_ready = sem("q_ready")
        k_ready = sem("k_ready")
        vt_ready = sem("vt_ready")
        v_ready = sem("v_ready")
        scores_ready = sem("scores_ready")
        pt_ready = sem("pt_ready")
        ctx_ready = sem("ctx_ready")
        out_ready = sem("out_ready")
        q_hi = sem("q_hi")
        k_hi = sem("k_hi")
        vt_copied = sem("vt_copied")
        v_hi_done = sem("v_hi_done")
        exp_done = sem("exp_done")
        pt_hi_done = sem("pt_hi_done")
        ctx_hi = sem("ctx_hi")
        abs_done = sem("abs_done")
        q_split = sem("q_split")
        k_split = sem("k_split")
        v_split = sem("v_split")
        masked = sem("masked")
        negmax_done = sem("negmax_done")
        rinv_done = sem("rinv_done")
        pt_split = sem("pt_split")
        ctx_split = sem("ctx_split")
        out_added = sem("out_added")
        abs_added = sem("abs_added")
        tot_done = sem("tot_done")
        step = sem("step")
        scales_done = sem("scales_done")
        pool_passed = sem("pool_passed")
        dve_passed = sem("dve_passed")
        normed = sem("normed")
        tot_ready = sem("tot_ready")
        bn_done = sem("bn_done")
        aggr_done = sem("aggr_done")
        stats_done = sem("stats_done")
        std_done = sem("std_done")
        rstd_done = sem("rstd_done")
        ln_done = sem("ln_done")
        x1t_ready = sem("x1t_ready")
        x1t_hi = sem("x1t_hi")
        x1t_split = sem("x1t_split")
        below_done = sem("below_done")
        tern_done = sem("tern_done")
        up_ready = sem("up_ready")
        gate_ready = sem("gate_ready")
        down_ready = sem("down_ready")
        silu_done = sem("silu_done")
        hid_done = sem("hid_done")
        hid_hi = sem("hid_hi")
        hid_split = sem("hid_split")
        down_added = sem("down_added")
        stored = sem("stored")

        first = ([("k", 0, 0)] + [("x", 0, k) for k in range(KT)] + [("q", 0, 0), ("v", 0, 0)]
                 + [("q", 0, h) for h in (1, 2, 3)] + [("x", b, k) for b in (1, 2, 3) for k in range(KT)])
        current = [("d", 0, h) for h in range(HPG)]
        ahead = [("k", 1, 0), ("q", 1, 0), ("v", 1, 0), ("q", 1, 1), ("q", 1, 2), ("q", 1, 3)]
        PER_G = len(current) + len(ahead)
        assert PER_G % RAW == 0
        N_FIRST = len(first)
        slot_of = {}
        landed_at = {}
        for m, piece in enumerate(first):
            slot_of["first", piece] = m % RAW
            landed_at["first", piece] = 16 * (m // RAW + 1)
        for m, piece in enumerate(current + ahead):
            slot_of["loop", piece] = (N_FIRST + m) % RAW
            landed_at["loop", piece] = 16 * ((N_FIRST + m) // RAW + 1)
        PER_SLOT = 16 * (PER_G // RAW)
        on_vector = ([("x", 0, k) for k in range(KT)] + [("k", 0, 0), ("q", 0, 0), ("v", 0, 0), ("q", 0, 1)])
        on_vector.sort(key=first.index)
        on_pool_x = [p for p in first if p[0] == "x" and p not in on_vector]
        on_pool_w = [p for p in first if p[0] != "x" and p not in on_vector]
        NW_FIRST = len(on_pool_w)

        def parts(piece):
            kind, i, j = piece
            at = slice(i * S, (i + 1) * S)
            return {"x": lambda: (xt_hi[:, j, at], xt_lo[:, j, at]),
                    "k": lambda: (wk_hi[:], wk_lo[:]), "v": lambda: (wv_hi[:], wv_lo[:]),
                    "q": lambda: (wa_hi[:, j, :], wa_lo[:, j, :]),
                    "d": lambda: (wd_hi[:, j, :], wd_lo[:, j, :])}[kind]()

        def after(i, n):
            return nc.s_assert_within(i + 1, 1, n - 1,
                                      skip_runtime_bounds_check_because="under If(i < n - 1)")

        def source(piece, g):
            kind, ahead_by, j = piece
            if kind == "x":
                return x_t[ahead_by, j]
            at = after(g, G) if ahead_by else g
            return {"k": w_k, "v": w_v}[kind][at] if kind in "kv" else {"q": w_q, "d": w_dense}[kind][at, j]

        START = 5

        block = ctx.enter_context(nc.Block())

        @block.sync
        def _(sp):
            def release(piece):
                if piece in on_vector:
                    sp.wait_ge(first_split, on_vector.index(piece) + 1)
                elif piece in on_pool_x:
                    sp.wait_ge(x_split_pool, on_pool_x.index(piece) + 1)
                else:
                    sp.wait_ge(w_split, on_pool_w.index(piece) + 1)

            for m, piece in enumerate(first):
                if m >= RAW:
                    release(first[m - RAW])
                sp.dma_start(raw[:, m % RAW, :], source(piece, 0)).then_inc(raw_landed[m % RAW], 16)
            for b in range(B):
                sp.dma_start(resid[:, b * QT:(b + 1) * QT, :], x_nat[b]).then_inc(resid_loaded, 16)

            for piece in first[-RAW:]:
                release(piece)
            with sp.Fori(0, G) as g:
                def load(m):
                    piece = (current + ahead)[m]
                    s = slot_of["loop", piece]
                    if m >= RAW:
                        sp.wait_ge(w_split, g * PER_G + NW_FIRST + m - RAW + 1)
                    sp.dma_start(raw[:, s, :], source(piece, g)).then_inc(raw_landed[s], 16)

                sp.wait_ge(w_split, g * PER_G + NW_FIRST)
                for m in range(len(current)):
                    load(m)
                with sp.If(g < G - 1):
                    for m in range(len(current), PER_G):
                        load(m)

            sp.wait_ge(abs_done, START + G * 3 * ET)
            order0 = [(w, et) for et in range(ET) for w in (0, 1)]
            for m, (w, et) in enumerate(order0):
                if m >= FRAW:
                    sp.wait_ge(tern_done, m - FRAW + 1)
                sp.dma_start(fraw[:, m % FRAW, :], (w_up, w_gate)[w][0, et]).then_inc(fraw_landed[m % FRAW], 16)
            with sp.Fori(0, C) as c:
                for m in range(3 * ET):
                    if m < ET:
                        sp.wait_ge(tern_done, c * 3 * ET + 2 * ET + m - FRAW + 1)
                        sp.dma_start(fraw[:, m % FRAW, :], w_down[c, m]).then_inc(fraw_landed[m % FRAW], 16)
                with sp.If(c < C - 1):
                    for m, (w, et) in enumerate(order0):
                        m += ET
                        sp.wait_ge(tern_done, c * 3 * ET + 2 * ET + m - FRAW + 1)
                        sp.dma_start(fraw[:, m % FRAW, :], (w_up, w_gate)[w][after(c, C), et]).then_inc(
                            fraw_landed[m % FRAW], 16)

            for b in range(B):
                sp.wait_ge(ln_done, B * QT + (b + 1) * QT)
                sp.dma_start(out_nat[b], resid[:, b * QT:(b + 1) * QT, :]).then_inc(stored, 16)
            sp.wait_ge(stored, 16 * B)

        @block.gpsimd
        def _(pool):
            nc.gpsimd.memset(mask[:], 0.0).then_inc(zeroed, 1)
            nc.gpsimd.memset(ident[:], 0.0).then_inc(zeroed, 1)
            nc.gpsimd.memset(ones[:], 1.0).then_inc(consts, 1)
            nc.gpsimd.memset(power[:], -0.5).then_inc(consts, 1)
            nc.gpsimd.memset(abs_tot[:], 0.0).then_inc(consts, 1)
            pool.wait_ge(zeroed, 2)
            nc.gpsimd.affine_select(out=mask[:, S - P:S], in_=mask[:, S - P:S], compare_op=ALU.is_ge, fill=NEG,
                                    base=0, pattern=[[-1, P]], channel_multiplier=1).then_inc(consts, 1)
            nc.gpsimd.affine_select(out=ident[:], in_=ident[:], compare_op=ALU.not_equal, fill=1.0,
                                    base=0, pattern=[[-1, P]], channel_multiplier=1).then_inc(consts, 1)

            def wait_apart():
                pool.sem_inc(pool_passed, 1)

            def round_to(dst, src):
                wide = ones[:, 0:P].unsqueeze(1).to_broadcast([P, 4, P])
                return nc.gpsimd.tensor_tensor(dst.rearrange("p (a b) -> p a b", b=P),
                                               src.rearrange("p (a b) -> p a b", b=P), wide, ALU.mult)

            pool.wait_ge(consts, 5)
            pool.sem_inc(wk_split, 1)
            pool.sem_inc(wv_split, 1)
            pool.sem_inc(wq_split, 2)

            def weight(piece, phase, base_landed, n_hi):
                s = slot_of[phase, piece]
                pool.wait_ge(raw_landed[s], base_landed + landed_at[phase, piece])
                hi, lo = parts(piece)
                done = {"k": wk_split, "v": wv_split, "q": wq_split, "d": wd_split}[piece[0]]
                wait_apart()
                round_to(hi, raw[:, s, :]).then_inc(w_hi_done, 1)
                pool.wait_ge(w_hi_done, n_hi)
                nc.gpsimd.tensor_tensor(lo, raw[:, s, :], hi.bitcast(F32), ALU.subtract).then_inc(w_split, 1)
                pool.wait_ge(w_split, n_hi)
                pool.sem_inc(done, 1)

            for m, piece in enumerate(on_pool_w):
                weight(piece, "first", 0, m + 1)
            for m, piece in enumerate(on_pool_x):
                s = slot_of["first", piece]
                pool.wait_ge(raw_landed[s], landed_at["first", piece])
                hi, lo = parts(piece)
                round_to(hi, raw[:, s, :]).then_inc(x_hi_pool, 1)
                pool.wait_ge(x_hi_pool, m + 1)
                nc.gpsimd.tensor_tensor(lo, raw[:, s, :], hi.bitcast(F32), ALU.subtract).then_inc(x_split_pool, 1)

            with pool.Fori(0, G) as g:
                for n in range(N):
                    if n in (2, 3):
                        pool.wait_ge(out_ready, START + g * N)
                        for m in (2 * (n - 2), 2 * (n - 2) + 1):
                            weight(current[m], "loop", g * PER_SLOT, g * PER_G + NW_FIRST + m + 1)
                    when = {12: (0, 1), 13: (2, 3), 14: (4,), 15: (5,)}
                    if n in when:
                        with pool.If(g < G - 1):
                            for m in when[n]:
                                kind, _, j = ahead[m]
                                if kind == "k":
                                    pool.wait_ge(k_ready, g * B + B)
                                elif kind == "v":
                                    pool.wait_ge(vt_ready, g * B + B)
                                else:
                                    pool.wait_ge(q_ready, g * N + N - HPG + j + 1)
                                weight(ahead[m], "loop", g * PER_SLOT, g * PER_G + NW_FIRST + 4 + m + 1)

            def one_over_std(batches):
                pool.wait_ge(stats_done, batches + 1)
                nc.gpsimd.tensor_scalar(std[:], mv[:, :, 1], LN_EPS, None, ALU.add).then_inc(std_done, 1)
                pool.wait_ge(std_done, batches + 1)
                nc.gpsimd.tensor_tensor(rstd[:], std[:], power[:], ALU.pow).then_inc(rstd_done, 1)

            for batches in range(2 * B):
                one_over_std(batches)

        @block.scalar
        def _(act):
            copy = nc.scalar.copy
            for s in (pt_hi_done, ctx_hi, abs_done):
                act.sem_inc(s, START)
            for m, piece in enumerate(on_vector):
                s = slot_of["first", piece]
                act.wait_ge(raw_landed[s], landed_at["first", piece])
                copy(parts(piece)[0], raw[:, s, :]).then_inc(first_hi, 1)
            act.wait_ge(k_ready, 1)
            copy(kt_hi[:], ps[:, OUT_BANK, :]).then_inc(k_hi, 1)
            act.wait_ge(q_ready, 1)
            copy(qt_hi[:], ps[:, Q_BANK, :]).then_inc(q_hi, 1)

            def pt_evacuate(head, chunk):
                _, at, w = PT_CHUNKS[chunk]
                act.wait_ge(pt_ready, START + head * 3 - 2 + chunk)
                copy(pt_hi[:, at:at + w], ps[:, PT_BANKS[chunk], 0:w]).then_inc(pt_hi_done, 1)

            def ctx_evacuate(head, b, h):
                act.wait_ge(ctx_ready, START + head)
                copy(mid_hi[:, b % 2, h, :], ps[:, CTX_BANK, :]).then_inc(ctx_hi, 1)

            def next_q(g, n):
                act.wait_ge(q_ready, g * N + n + 2)
                copy(qt_hi[:], ps[:, Q_BANK, :]).then_inc(q_hi, 1)

            def next_k(g, b):
                act.wait_ge(k_ready, g * B + b + 2)
                copy(kt_hi[:], ps[:, OUT_BANK, :]).then_inc(k_hi, 1)

            def load_ffn(at, n):
                which, et = divmod(n, ET)
                act.dma_start(fraw[:, n % FRAW, :], (w_up, w_gate, w_down)[which][at, et]).then_inc(
                    fraw_landed[n % FRAW], 16)

            for n in range(FRAW - 1):
                load_ffn(0, n)
            with act.Fori(0, G) as g:
                for n in range(N):
                    b, h = divmod(n, HPG)
                    before = (b, h - 1) if h else ((b - 1) % B, HPG - 1)
                    if n:
                        pt_evacuate(g * N + n, 0)
                        pt_evacuate(g * N + n, 1)
                    else:
                        with act.If(g > 0):
                            pt_evacuate(g * N + n, 0)
                            pt_evacuate(g * N + n, 1)
                    if n:
                        pt_evacuate(g * N + n, 2)
                    else:
                        with act.If(g > 0):
                            pt_evacuate(g * N + n, 2)
                    act.wait_ge(negmax_done, g * N + n + 1)
                    for i in TILE_ORDER:
                        t = probs[:, n % 2, S_SBUF[i]:S_SBUF[i] + P * (i + 1)]
                        nc.scalar.activation(t, t, ACT.Exp, bias=negmax[:, n % 2, i:i + 1], scale=SCALE,
                                             accum_out=rowsum[:, n % 2, i:i + 1]).then_inc(exp_done, 1)
                    if n < N - 1:
                        next_q(g, n)
                    else:
                        with act.If(g < G - 1):
                            next_q(g, n)
                    if h == 3:
                        if b < B - 1:
                            next_k(g, b)
                        else:
                            with act.If(g < G - 1):
                                next_k(g, b)
                    if h == 0:
                        act.wait_ge(vt_ready, g * B + b + 1)
                        copy(vt[:], ps[:, OUT_BANK, :]).then_inc(vt_copied, 1)
                    if n:
                        ctx_evacuate(g * N + n, *before)
                    else:
                        with act.If(g > 0):
                            ctx_evacuate(g * N + n, *before)
                    if h == 0:
                        act.wait_ge(v_ready, g * B + b + 1)
                        copy(v_hi[:], ps[:, OUT_BANK, :]).then_inc(v_hi_done, 1)
                    if n < 3 * ET:
                        which, et = divmod(n, ET)
                        s = n % FRAW
                        act.wait_ge(fraw_landed[s], g * 16 * (3 * ET // FRAW) + 16 * (n // FRAW + 1))
                        act.wait_ge(abs_added, START + g)
                        nc.scalar.activation(fraw[:, s, :], fraw[:, s, :], ACT.Abs,
                                             accum_out=abs_part[:, which, et:et + 1]).then_inc(abs_done, 1)
                        if n + FRAW - 1 < 3 * ET:
                            act.wait_ge(abs_done, START + g * 3 * ET + n)
                            load_ffn(g, n + FRAW - 1)
                        else:
                            with act.If(g < G - 1):
                                act.wait_ge(abs_done, START + g * 3 * ET + n)
                                load_ffn(after(g, G), n + FRAW - 1 - 3 * ET)
            for chunk in range(3):
                pt_evacuate(G * N, chunk)
            ctx_evacuate(G * N, B - 1, HPG - 1)

            def x1_transposed(b):
                for k in range(KT):
                    act.wait_ge(x1t_ready, b * KT + k + 1)
                    copy(xt_hi[:, k, b * S:(b + 1) * S], ps[:, LN_BANK + k % 2, :]).then_inc(x1t_hi, 1)

            x1_transposed(0)
            with act.Fori(0, C) as c:
                for u in range(N):
                    b, et = divmod(u, ET)
                    act.wait_ge(up_ready, c * N + u + 1)
                    if u >= 2:
                        act.wait_ge(hid_done, START + c * N + u - 1)
                    nc.scalar.activation(sil[:, u % 2, :], ps[:, UP_BANK + u % 2, :], ACT.Silu,
                                         scale=scales[:, 0:1]).then_inc(silu_done, 1)
                    act.wait_ge(hid_done, START + c * N + u + 1)
                    copy(mid_hi[:, b % 2, et, :], hid[:, u % 2, :]).then_inc(hid_hi, 1)
                    if et == 1 and b < B - 1:
                        with act.If(c < 1):
                            x1_transposed(b + 1)

        @block.vector
        def _(dve):
            for s in (pt_split, ctx_split, out_added, down_added, masked, normed, v_split, abs_added, hid_done, hid_split):
                dve.sem_inc(s, START)
            links = [0]

            def link(ins):
                links[0] += 1
                ins.then_inc(step, 1)
                dve.wait_ge(step, links[0])

            def low(lo, src, hi):
                return nc.vector.tensor_tensor(lo, src, hi.bitcast(F32), ALU.subtract)

            for m, piece in enumerate(on_vector):
                hi, lo = parts(piece)
                dve.wait_ge(first_hi, m + 1)
                low(lo, raw[:, slot_of["first", piece], :], hi).then_inc(first_split, 1)
            dve.wait_ge(k_hi, 1)
            low(kt_lo[:], ps[:, OUT_BANK, :], kt_hi[:]).then_inc(k_split, 1)
            dve.wait_ge(q_hi, 1)
            low(qt_lo[:], ps[:, Q_BANK, :], qt_hi[:]).then_inc(q_split, 1)
            dve.wait_ge(consts, 5)

            def pt_low(head, chunk):
                _, at, w = PT_CHUNKS[chunk]
                dve.wait_ge(pt_hi_done, START + head * 3 - 2 + chunk)
                low(pt_lo[:, at:at + w], ps[:, PT_BANKS[chunk], 0:w], pt_hi[:, at:at + w]).then_inc(pt_split, 1)

            def ctx_low(head, b, h):
                dve.wait_ge(ctx_hi, START + head)
                low(mid_lo[:, b % 2, h, :], ps[:, CTX_BANK, :], mid_hi[:, b % 2, h, :]).then_inc(ctx_split, 1)

            def next_q(g, n):
                dve.wait_ge(q_hi, g * N + n + 2)
                low(qt_lo[:], ps[:, Q_BANK, :], qt_hi[:]).then_inc(q_split, 1)

            def next_k(g, b):
                dve.wait_ge(k_hi, g * B + b + 2)
                low(kt_lo[:], ps[:, OUT_BANK, :], kt_hi[:]).then_inc(k_split, 1)

            def add_out(tiles, b, t):
                dve.wait_ge(out_ready, START + tiles)
                dve.wait_ge(resid_loaded, 16 * B)
                r = resid[:, b * QT + t, :]
                nc.vector.tensor_tensor(r, ps[:, OUT_BANK, :], r, ALU.add).then_inc(out_added, 1)

            with dve.Fori(0, G) as g:
                for n in range(N):
                    b, h = divmod(n, HPG)
                    before = (b, h - 1) if h else ((b - 1) % B, HPG - 1)
                    if n:
                        pt_low(g * N + n, 0)
                        pt_low(g * N + n, 1)
                    else:
                        with dve.If(g > 0):
                            pt_low(g * N + n, 0)
                            pt_low(g * N + n, 1)
                    for a, i in enumerate(TILE_ORDER):
                        w = P * (i + 1)
                        if a != 1:
                            dve.wait_ge(scores_ready, (g * N + n) * 3 + max(a, 1))
                            dve.sem_inc(dve_passed, 1)
                        nc.vector.tensor_tensor_reduce(
                            out=probs[:, n % 2, S_SBUF[i]:S_SBUF[i] + w], in0=flat[:, S_PSUM[i]:S_PSUM[i] + w],
                            in1=mask[:, S - w:S], scale=1.0, scalar=NEG, op0=ALU.add, op1=ALU.max,
                            accum_out=rowmax[:, n % 2, i:i + 1]).then_inc(masked, 1)
                    dve.wait_ge(masked, START + (g * N + n) * 4 + 4)
                    nc.vector.tensor_scalar(negmax[:, n % 2, :], rowmax[:, n % 2, :], -SCALE, None,
                                            ALU.mult).then_inc(negmax_done, 1)
                    if n:
                        pt_low(g * N + n, 2)
                    else:
                        with dve.If(g > 0):
                            pt_low(g * N + n, 2)
                    tiles = {1: (0, 1), 2: (2, 3)}.get(h)
                    if tiles:
                        if b:
                            add_out(g * N + (b - 1) * QT + tiles[0] + 1, b - 1, tiles[0])
                        else:
                            with dve.If(g > 0):
                                add_out(g * N - QT + tiles[0] + 1, B - 1, tiles[0])
                    if n < N - 1:
                        next_q(g, n)
                    else:
                        with dve.If(g < G - 1):
                            next_q(g, n)
                    dve.wait_ge(exp_done, (g * N + n) * 4 + 4)
                    nc.vector.reciprocal(rinv[:, n % 2, :], rowsum[:, n % 2, :]).then_inc(rinv_done, 1)
                    dve.wait_ge(rinv_done, g * N + n + 1)
                    for i in TILE_ORDER:
                        t = probs[:, n % 2, S_SBUF[i]:S_SBUF[i] + P * (i + 1)]
                        nc.vector.tensor_scalar(t, t, rinv[:, n % 2, i:i + 1], None, ALU.mult).then_inc(normed, 1)
                    if tiles:
                        if b:
                            add_out(g * N + (b - 1) * QT + tiles[1] + 1, b - 1, tiles[1])
                        else:
                            with dve.If(g > 0):
                                add_out(g * N - QT + tiles[1] + 1, B - 1, tiles[1])
                    if h == 3:
                        if b < B - 1:
                            next_k(g, b)
                        else:
                            with dve.If(g < G - 1):
                                next_k(g, b)
                    if n:
                        ctx_low(g * N + n, *before)
                    else:
                        with dve.If(g > 0):
                            ctx_low(g * N + n, *before)
                    if h == 0:
                        dve.wait_ge(v_hi_done, g * B + b + 1)
                        low(v_lo[:], ps[:, OUT_BANK, :], v_hi[:]).then_inc(v_split, 1)
                dve.wait_ge(abs_done, START + (g + 1) * 3 * ET)
                dve.wait_ge(abs_added, START + g)
                nc.vector.tensor_tensor(abs_tot[:], abs_tot[:], abs_part[:], ALU.add).then_inc(abs_added, 1)

            dve.wait_ge(abs_added, START + G)
            nc.vector.tensor_reduce(abs_sum[:, 0:3], abs_tot[:], mybir.AxisListType.X, ALU.add).then_inc(tot_done, 1)
            dve.wait_ge(tot_ready, 1)
            link(nc.vector.tensor_scalar(scales[:, 0:3], ps[:, UP_BANK, 0:3], 1.0 / (D * E), QUANT_EPS, ALU.mult, ALU.add))
            link(nc.vector.tensor_scalar(thr[:, 0:3], scales[:, 0:3], 0.5, None, ALU.mult))
            link(nc.vector.tensor_scalar(nthr[:, 0:3], scales[:, 0:3], -0.5, None, ALU.mult))
            link(nc.vector.tensor_tensor(scales[:, 3:4], scales[:, 1:2], scales[:, 2:3], ALU.mult))
            dve.sem_inc(scales_done, 1)

            for chunk in range(3):
                pt_low(G * N, chunk)
            ctx_low(G * N, B - 1, HPG - 1)

            def take_stats(b, t):
                nc.vector.bn_stats(stats[:, t, :], resid[:, b * QT + t, :]).then_inc(bn_done, 1)

            def layer_norm(b, batches):
                dve.wait_ge(bn_done, (batches + 1) * QT)
                for t in range(QT):
                    nc.vector.bn_aggr(mv[:, t, :], stats[:, t, :]).then_inc(aggr_done, 1)
                dve.wait_ge(aggr_done, (batches + 1) * QT)
                dve.sem_inc(stats_done, 1)
                dve.wait_ge(rstd_done, batches + 1)
                for t in range(QT):
                    r = resid[:, b * QT + t, :]
                    nc.vector.tensor_scalar(r, r, mv[:, t, 0:1], rstd[:, t:t + 1], ALU.subtract,
                                            ALU.mult).then_inc(ln_done, 1)

            def x1_transposed(b):
                for k in range(KT):
                    dve.wait_ge(x1t_hi, b * KT + k + 1)
                    low(xt_lo[:, k, b * S:(b + 1) * S], ps[:, LN_BANK + k % 2, :],
                        xt_hi[:, k, b * S:(b + 1) * S]).then_inc(x1t_split, 1)

            def ternary(which, et, base, m, pieces):
                src = fraw[:, m % FRAW, :]
                dst = (wa_hi, wa_lo, wd_hi)[which][:, et, :]
                dve.wait_ge(fraw_landed[m % FRAW], base + LANDED0 + 16 * (m // FRAW + 1))
                if m:
                    dve.wait_ge(tern_done, pieces)
                nc.vector.tensor_scalar(vt[:], src, nthr[:, which:which + 1], None, ALU.is_lt).then_inc(below_done, 1)
                dve.wait_ge(below_done, pieces + 1)
                nc.vector.scalar_tensor_tensor(dst, src, thr[:, which:which + 1], vt[:], ALU.is_gt,
                                               ALU.subtract).then_inc(tern_done, 1)

            LANDED0 = 16 * (G * 3 * ET // FRAW)
            dve.wait_ge(q_ready, G * N)
            dve.wait_ge(v_ready, G * B)
            dve.wait_ge(out_added, START + (G - 1) * N + QT)
            for t in range(QT):
                take_stats(0, t)
            layer_norm(0, 0)
            for t in range(QT):
                add_out(G * N - QT + t + 1, B - 1, t)
                if t == 1:
                    x1_transposed(0)
                for w in (0, 1):
                    ternary(w, t, 0, 2 * t + w, 2 * t + w)

            def add_down(tiles, b, t):
                dve.wait_ge(down_ready, START + tiles)
                r = resid[:, b * QT + t, :]
                nc.vector.scalar_tensor_tensor(r, ps[:, DOWN_BANK + t % 2, :], scales[:, 3:4], r,
                                               ALU.mult, ALU.add).then_inc(down_added, 1)

            with dve.Fori(0, C) as c:
                PER_C = 16 * (3 * ET // FRAW)
                for u in range(N):
                    b, et = divmod(u, ET)
                    dve.wait_ge(silu_done, c * N + u + 1)
                    dve.wait_ge(gate_ready, c * N + u + 1)
                    if u >= 2:
                        dve.wait_ge(hid_split, START + c * N + u - 1)
                    nc.vector.tensor_tensor(hid[:, u % 2, :], ps[:, GATE_BANK + u % 2, :], sil[:, u % 2, :],
                                            ALU.mult).then_inc(hid_done, 1)
                    for t in {1: (0, 1), 2: (2, 3)}.get(et, ()):
                        if b:
                            add_down(c * N + (b - 1) * QT + t + 1, b - 1, t)
                        else:
                            with dve.If(c > 0):
                                add_down(c * N - QT + t + 1, B - 1, t)
                    dve.wait_ge(hid_hi, c * N + u + 1)
                    low(mid_lo[:, b % 2, et, :], hid[:, u % 2, :], mid_hi[:, b % 2, et, :]).then_inc(hid_split, 1)
                    if et == 0 and b < B - 1:
                        with dve.If(c < 1):
                            dve.wait_ge(out_added, START + (G - 1) * N + (b + 2) * QT)
                            for t in range(QT):
                                take_stats(b + 1, t)
                            layer_norm(b + 1, b + 1)
                    if et == 1 and b < B - 1:
                        with dve.If(c < 1):
                            x1_transposed(b + 1)
                    if u == 2:
                        dve.wait_ge(down_ready, START + c * N)
                        for e in range(ET):
                            m = 2 * ET + e
                            ternary(2, e, c * PER_C, m, c * 3 * ET + m)
                    if b == B - 1:
                        with dve.If(c < C - 1):
                            dve.wait_ge(gate_ready, c * N + u + 1)
                            for w in (0, 1):
                                m = 3 * ET + 2 * et + w
                                ternary(w, et, c * PER_C, m, c * 3 * ET + m)
                    if et == 3 and b:
                        with dve.If(c > C - 2):
                            dve.wait_ge(down_added, START + c * N + b * QT)
                            for t in range(QT):
                                take_stats(b - 1, t)
                            layer_norm(b - 1, B + b - 1)
            for t in range(QT):
                add_down(C * N - QT + t + 1, B - 1, t)
                dve.wait_ge(down_added, START + C * N - QT + t + 1)
                take_stats(B - 1, t)
            layer_norm(B - 1, 2 * B - 1)

        @block.tensor
        def _(pe):
            mm = nc.tensor.matmul
            for s in (pt_ready, out_ready, down_ready, ctx_ready):
                pe.sem_inc(s, START)

            def product(bank_ap, terms):
                for n, (w, v) in enumerate(terms):
                    last = mm(bank_ap, w, v, start=n == 0, stop=n == len(terms) - 1)
                return last

            def project(bank, w_hi, w_lo, b):
                at = slice(b * S, (b + 1) * S)
                return product(ps[:, bank, :], [
                    t for k in range(KT) for t in (
                        (w_hi[:, k * P:(k + 1) * P], xt_hi[:, k, at]),
                        (w_hi[:, k * P:(k + 1) * P], xt_lo[:, k, at]),
                        (w_lo[:, k * P:(k + 1) * P], xt_hi[:, k, at]))])

            def x_of(b):
                pe.wait_ge(x_split_pool, b * KT)

            def q_project(b, h):
                project(Q_BANK, wa_hi[:, h, :], wa_lo[:, h, :], b).then_inc(q_ready, 1)

            def k_project(b):
                project(OUT_BANK, wk_hi[:], wk_lo[:], b).then_inc(k_ready, 1)

            def transpose_chunk(par, chunk):
                js, _, _ = PT_CHUNKS[chunk]
                at = 0
                for j in js:
                    for i in range(j, QT):
                        last = nc.tensor.transpose(ps[:, PT_BANKS[chunk], at:at + P],
                                                   probs[:, par, S_SBUF[i] + j * P:S_SBUF[i] + (j + 1) * P], ident[:])
                        at += P
                last.then_inc(pt_ready, 1)

            def transposes_ab(heads, par):
                pe.wait_ge(normed, START + heads * 4 + 4)
                pe.wait_ge(pt_split, START + heads * 3)
                transpose_chunk(par, 0)
                transpose_chunk(par, 1)

            def transposes_c(heads, par):
                pe.wait_ge(pt_split, START + heads * 3 + 1)
                transpose_chunk(par, 2)

            def pv(heads, batches):
                pe.wait_ge(pt_split, START + heads * 3 + 3)
                pe.wait_ge(v_split, START + batches)
                pe.wait_ge(ctx_split, START + heads)
                n = 0
                for j in (0, 1, 3, 2):
                    w = S - j * P
                    at = PT_AT[j]
                    for v, p in ((v_hi, pt_hi), (v_hi, pt_lo), (v_lo, pt_hi)):
                        last = mm(ps[:, CTX_BANK, j * P:S], v[:, j * P:(j + 1) * P], p[:, at:at + w],
                                  start=n == 0, stop=n == 3 * QT - 1)
                        n += 1
                last.then_inc(ctx_ready, 1)

            def out_tile(tiles, par, t):
                pe.wait_ge(out_added, START + tiles)
                at = slice(t * P, (t + 1) * P)
                product(ps[:, OUT_BANK, :], [
                    t for h in range(HPG) for t in (
                        (mid_hi[:, par, h, at], wd_hi[:, h, :]),
                        (mid_hi[:, par, h, at], wd_lo[:, h, :]),
                        (mid_lo[:, par, h, at], wd_hi[:, h, :]))]).then_inc(out_ready, 1)

            need = {p: n + 1 for n, p in enumerate(on_vector)}
            for k in range(KT):
                pe.wait_ge(first_split, need["x", 0, k])
                at = slice(k * P, (k + 1) * P)
                for n, (w, v) in enumerate(((wk_hi, xt_hi), (wk_hi, xt_lo), (wk_lo, xt_hi))):
                    last = mm(ps[:, OUT_BANK, :], w[:, at], v[:, k, 0:S], start=k + n == 0,
                              stop=k == KT - 1 and n == 2)
            last.then_inc(k_ready, 1)
            pe.wait_ge(first_split, need["q", 0, 0])
            q_project(0, 0)
            pe.wait_ge(first_split, len(on_vector))
            pe.wait_ge(consts, 5)

            with pe.Fori(0, G) as g:
                for n in range(N):
                    b, h = divmod(n, HPG)
                    if n:
                        transposes_ab(g * N + n - 1, (n - 1) % 2)
                    else:
                        with pe.If(g > 0):
                            transposes_ab(g * N + n - 1, (n - 1) % 2)

                    pe.wait_ge(q_split, g * N + n + 1)
                    if h == 0:
                        pe.wait_ge(k_split, g * B + b + 1)
                    pe.wait_ge(masked, START + (g * N + n) * 4)
                    for i in TILE_ORDER:
                        at, w = slice(i * P, (i + 1) * P), P * (i + 1)
                        last = product(flat[:, S_PSUM[i]:S_PSUM[i] + w], [
                            (qt_hi[:, at], kt_hi[:, 0:w]), (qt_hi[:, at], kt_lo[:, 0:w]), (qt_lo[:, at], kt_hi[:, 0:w])])
                        if i:
                            last.then_inc(scores_ready, 1)

                    if n:
                        transposes_c(g * N + n - 1, (n - 1) % 2)
                    else:
                        with pe.If(g > 0):
                            transposes_c(g * N + n - 1, (n - 1) % 2)

                    tiles = {1: (0, 1), 2: (2, 3)}.get(h)

                    def out_of_batch_before(t, first):
                        if b:
                            if first:
                                pe.wait_ge(ctx_split, START + g * N + b * HPG)
                                pe.wait_ge(v_split, START + g * B + b + 1)
                                if b == 1:
                                    pe.wait_ge(wd_split, (g + 1) * HPG)
                            out_tile(g * N + (b - 1) * QT + t, (b - 1) % 2, t)
                        else:
                            with pe.If(g > 0):
                                if first:
                                    pe.wait_ge(ctx_split, START + g * N)
                                    pe.wait_ge(v_split, START + g * B + b + 1)
                                out_tile(g * N - QT + t, (B - 1) % 2, t)

                    if tiles:
                        out_of_batch_before(tiles[0], h == 1)

                    def next_q():
                        nb, nh = divmod((n + 1) % N, HPG)
                        if nh == 0:
                            x_of(nb)
                        if nb == 0:
                            pe.wait_ge(wq_split, (g + (1 if n == N - 1 else 0)) * HPG + nh + 1)
                        q_project(nb, nh)
                    if n < N - 1:
                        next_q()
                    else:
                        with pe.If(g < G - 1):
                            next_q()

                    if tiles:
                        out_of_batch_before(tiles[1], False)
                    if h == 3:
                        if b < B - 1:
                            pe.wait_ge(out_added, START + g * N + b * QT)
                            k_project(b + 1)
                        else:
                            with pe.If(g < G - 1):
                                pe.wait_ge(out_added, START + g * N + b * QT)
                                pe.wait_ge(wk_split, g + 2)
                                k_project(0)
                    if h == 0:
                        if b == 0:
                            pe.wait_ge(wv_split, g + 1)
                        project(OUT_BANK, wv_hi[:], wv_lo[:], b).then_inc(vt_ready, 1)

                    def pv_before():
                        pv(g * N + n - 1, g * B + (b if h else b - 1) + 1)
                    if n:
                        pv_before()
                    else:
                        with pe.If(g > 0):
                            pv(g * N - 1, g * B)
                    if h == 0:
                        pe.wait_ge(vt_copied, g * B + b + 1)
                        for t in range(QT):
                            last = nc.tensor.transpose(ps[:, OUT_BANK, t * P:(t + 1) * P], vt[:, t * P:(t + 1) * P], ident[:])
                        last.then_inc(v_ready, 1)

            transposes_ab(G * N - 1, (N - 1) % 2)
            pe.wait_ge(tot_done, 1)
            mm(ps[:, UP_BANK, 0:3], ones[:], abs_sum[:, 0:3], start=True, stop=True).then_inc(tot_ready, 1)
            transposes_c(G * N - 1, (N - 1) % 2)
            pv(G * N - 1, G * B)
            pe.wait_ge(ctx_split, START + G * N)

            def x1_transposed(b):
                pe.wait_ge(ln_done, (b + 1) * QT)
                for k in range(KT):
                    if b * KT + k >= 2:
                        pe.wait_ge(x1t_split, b * KT + k - 1)
                    for t in range(QT):
                        last = nc.tensor.transpose(ps[:, LN_BANK + k % 2, t * P:(t + 1) * P],
                                                   resid[:, b * QT + t, k * P:(k + 1) * P], ident[:])
                    last.then_inc(x1t_ready, 1)

            for t in range(QT):
                out_tile(G * N - QT + t, (B - 1) % 2, t)
                if t == 1:
                    x1_transposed(0)

            def half(bank, w, b):
                at = slice(b * S, (b + 1) * S)
                return product(ps[:, bank, :], [
                    (w[:, k * P:(k + 1) * P], v[:, k, at]) for k in range(KT) for v in (xt_hi, xt_lo)])

            def down_tile(tiles, par, t):
                if t < 2:
                    pe.wait_ge(down_added, START + tiles - t)
                else:
                    pe.wait_ge(down_added, START + tiles - 1)
                at = slice(t * P, (t + 1) * P)
                product(ps[:, DOWN_BANK + t % 2, :], [
                    (v[:, par, et, at], wd_hi[:, et, :]) for et in range(ET) for v in (mid_hi, mid_lo)
                ]).then_inc(down_ready, 1)

            with pe.Fori(0, C) as c:
                for u in range(N):
                    b, et = divmod(u, ET)
                    if et == 0:
                        pe.wait_ge(x1t_split, (b + 1) * KT)
                    if u >= 2:
                        pe.wait_ge(hid_done, START + c * N + u - 1)
                    else:
                        pe.wait_ge(hid_done, START + c * N)
                    if b == 0:
                        pe.wait_ge(tern_done, c * 3 * ET + 2 * et + 2)
                    half(UP_BANK + u % 2, wa_hi[:, et, :], b).then_inc(up_ready, 1)
                    half(GATE_BANK + u % 2, wa_lo[:, et, :], b).then_inc(gate_ready, 1)
                    for t in {1: (0, 1), 2: (2, 3)}.get(et, ()):
                        if b:
                            if t == 0:
                                pe.wait_ge(hid_split, START + c * N + b * ET)
                                if b == 1:
                                    pe.wait_ge(tern_done, (c + 1) * 3 * ET)
                            down_tile(c * N + (b - 1) * QT + t, (b - 1) % 2, t)
                        else:
                            with pe.If(c > 0):
                                if t == 0:
                                    pe.wait_ge(hid_split, START + c * N)
                                down_tile(c * N - QT + t, (B - 1) % 2, t)
                    if et == 1 and b < B - 1:
                        with pe.If(c < 1):
                            x1_transposed(b + 1)
            pe.wait_ge(hid_split, START + C * N)
            for t in range(QT):
                down_tile(C * N - QT + t, (B - 1) % 2, t)


def kernel(**inputs):
    import numpy as np
    import concourse.bacc as bacc
    from concourse.bass_utils import run_bass_kernel_spmd as run

    x = np.ascontiguousarray(inputs["L0_attn_x"])
    w_kv = inputs["L0_attn_w_kv"]

    def by_column(w, n):
        return np.ascontiguousarray(np.asarray(w).reshape(KT, P, n, P).transpose(2, 1, 0, 3).reshape(n, P, KT * P))

    arrays = {
        "x": x,
        "x_t": np.ascontiguousarray(np.asarray(x).transpose(0, 2, 1).reshape(B, KT, P, S)),
        "w_q": by_column(inputs["L0_attn_w_q"], G * HPG).reshape(G, HPG, P, KT * P),
        "w_k": by_column(w_kv[:, :G * DH], G),
        "w_v": by_column(w_kv[:, G * DH:], G),
        "w_dense": np.ascontiguousarray(inputs["L0_attn_w_dense"]).reshape(G, HPG, P, D),
        "w_up": by_column(np.asarray(inputs["L0_ffn_W_up"]).T, C * ET).reshape(C, ET, P, KT * P),
        "w_gate": by_column(np.asarray(inputs["L0_ffn_W_gate"]).T, C * ET).reshape(C, ET, P, KT * P),
        "w_down": np.ascontiguousarray(np.asarray(inputs["L0_ffn_W_down"]).T).reshape(C, ET, P, D),
    }
    nc = bacc.Bacc("TRN2", target_bir_lowering=False, num_devices=1, dynamic_dma_scratch_size=1024)
    args = [nc.dram_tensor(f"in_{name}", a.shape, mybir.dt.from_np(a.dtype), kind="ExternalInput").ap()
            for name, a in arrays.items()]
    args.append(nc.dram_tensor("out", (B, S, D), F32, kind="ExternalOutput").ap())
    layer(nc, *args)
    r = run(nc, [{f"in_{name}": a for name, a in arrays.items()}], core_ids=[0])
    return r.results[0]["out"]
```

```python
from contextlib import ExitStack

import concourse.bass as bass
from concourse import mybir

F32 = mybir.dt.float32
F32R = mybir.dt.float32r
ALU = mybir.AluOpType
ACT = mybir.ActivationFunctionType

P = 128
B = 4
S = 512
D = 512
KT = D // P
G = 4
HPG = 4
DH = 128
E = 2048
C = 4
ET = E // C // P
QT = S // P
N = B * HPG
SCALE = DH ** -0.5
LN_EPS = 1e-5
QUANT_EPS = 1e-8
WARM_UP = 10
NEG = -3.0e38

TILE_ORDER = (0, 1, 2, 3)
S_PSUM = {1: 0, 0: 256, 2: 512, 3: 1024}
S_SBUF = {0: 0, 2: 128, 1: 512, 3: 768}
PW = 1280
PT_AT = {0: 0, 1: 512, 3: 896, 2: 1024}
PT_CHUNKS = (((0,), 0, 512), ((1, 3), 512, 512), ((2,), 1024, 256))

RAW = 5
FRAW = 4


def layer(nc, x, x_t, w_q, w_k, w_v, w_dense, w_up, w_gate, w_down, out):
    with ExitStack() as ctx:
        def sb(name, shape, dt=F32):
            return ctx.enter_context(nc.sbuf_tensor(name, shape, dt))

        def sem(name):
            return ctx.enter_context(nc.semaphore(name))

        xt_hi = sb("xt_hi", [P, KT, B * S], F32R)
        xt_lo = sb("xt_lo", [P, KT, B * S], F32R)
        resid = sb("resid", [P, B * QT, D])
        wa_hi = sb("wa_hi", [P, HPG, KT * P], F32R)
        wa_lo = sb("wa_lo", [P, HPG, KT * P], F32R)
        wd_hi = sb("wd_hi", [P, HPG, D], F32R)
        wd_lo = sb("wd_lo", [P, HPG, D], F32R)
        wk_hi = sb("wk_hi", [P, KT * P], F32R)
        wk_lo = sb("wk_lo", [P, KT * P], F32R)
        wv_hi = sb("wv_hi", [P, KT * P], F32R)
        wv_lo = sb("wv_lo", [P, KT * P], F32R)
        raw = sb("raw", [P, RAW, 512])
        fraw = sb("fraw", [P, FRAW, 512])
        qt_hi = sb("qt_hi", [P, S], F32R)
        qt_lo = sb("qt_lo", [P, S], F32R)
        kt = sb("kt", [P, 2, S], F32R)
        vt = sb("vt", [P, S])
        v_hi = sb("v_hi", [P, S], F32R)
        v_lo = sb("v_lo", [P, S], F32R)
        probs = sb("probs", [P, 2, PW])
        pt_hi = sb("pt_hi", [P, PW], F32R)
        pt_lo = sb("pt_lo", [P, PW], F32R)
        mid_hi = sb("mid_hi", [P, 2, HPG, S], F32R)
        mid_lo = sb("mid_lo", [P, 2, HPG, S], F32R)
        mask = sb("mask", [P, S], mybir.dt.bfloat16)
        ident = sb("ident", [P, P])
        ones = sb("ones", [P, P])
        rowmax = sb("rowmax", [P, 2, QT])
        negmax = sb("negmax", [P, 2, QT])
        rowsum = sb("rowsum", [P, 2, QT])
        rinv = sb("rinv", [P, 2, QT])
        abs_part = sb("abs_part", [P, 3, ET])
        abs_tot = sb("abs_tot", [P, 3, ET])
        abs_sum = sb("abs_sum", [P, 4])
        scales = sb("scales", [P, 4])
        thr = sb("thr", [P, 4])
        nthr = sb("nthr", [P, 4])
        stats = sb("stats", [P, QT, 6])
        mv = sb("mv", [P, QT, 2])
        std = sb("std", [P, QT])
        rstd = sb("rstd", [P, QT])
        power = sb("power", [P, QT])

        ps = ctx.enter_context(nc.psum_tensor("ps", [P, 8, 512], F32))
        flat = ps[:, :, :].rearrange("p a b -> p (a b)")
        PT_BANKS, Q_BANK, CTX_BANK, OUT_BANK = (3, 4, 3), 5, 6, 7
        UP_BANKS, GATE_BANKS, DOWN_BANKS, X1_BANKS = (7, 0), (5, 2), (6, 1, 3, 4), (3, 4)
        TOT = ps[:, CTX_BANK, 0:3]

        x1_tiles = [(b, k) for b in range(B) for k in range(KT)]
        early_x1 = {9: 0, 10: 1, 11: 2, 12: 3, 14: 4, 15: 5}
        N_EARLY = len(early_x1)
        late_x1 = {ET: (8, 9), ET + 1: (10, 11), 2 * ET + 1: (12, 13), 2 * ET + 2: (14, 15)}

        def x1_at(m):
            b, k = x1_tiles[m]
            return k, slice(b * S, (b + 1) * S), CTX_BANK if m < N_EARLY else X1_BANKS[m % 2]

        sil = probs[:, 0, 0:1024].rearrange("p (a s) -> p a s", a=2)
        hid = [raw[:, n, :] for n in (0, 1)]
        below = [raw[:, n, :] for n in (2, 3, 4)]

        x_nat = x.rearrange("b (t p) d -> b p t d", p=P)
        out_nat = out.rearrange("b (t p) d -> b p t d", p=P)

        raw_landed = [sem(f"raw_landed{i}") for i in range(RAW)]
        fraw_landed = [sem(f"fraw_landed{i}") for i in range(FRAW)]
        resid_loaded = sem("resid_loaded")
        zeroed = sem("zeroed")
        ones_set = sem("ones_set")
        consts = sem("consts")
        first_hi = sem("first_hi")
        first_split = sem("first_split")
        x_hi_pool = sem("x_hi_pool")
        x_split_pool = sem("x_split_pool")
        w_hi_done = sem("w_hi_done")
        wk_split = sem("wk_split")
        wq_split = sem("wq_split")
        wv_split = sem("wv_split")
        wd_split = sem("wd_split")
        w_split = sem("w_split")
        q_ready = sem("q_ready")
        k_ready = sem("k_ready")
        vt_ready = sem("vt_ready")
        v_ready = sem("v_ready")
        scores_ready = sem("scores_ready")
        pt_ready = sem("pt_ready")
        ctx_ready = sem("ctx_ready")
        out_ready = sem("out_ready")
        q_hi = sem("q_hi")
        k_hi = sem("k_hi")
        vt_copied = sem("vt_copied")
        v_hi_done = sem("v_hi_done")
        exp_done = sem("exp_done")
        pt_hi_done = sem("pt_hi_done")
        ctx_hi = sem("ctx_hi")
        abs_done = sem("abs_done")
        q_split = sem("q_split")
        k_split = sem("k_split")
        v_split = sem("v_split")
        masked = sem("masked")
        tile0_masked = sem("tile0_masked")
        negmax_done = sem("negmax_done")
        rinv_done = sem("rinv_done")
        normed = sem("normed")
        pt_split = sem("pt_split")
        ctx_split = sem("ctx_split")
        out_added = sem("out_added")
        abs_added = sem("abs_added")
        tot_done = sem("tot_done")
        step = sem("step")
        pool_passed = sem("pool_passed")
        dve_passed = sem("dve_passed")
        tot_ready = sem("tot_ready")
        bn_done = sem("bn_done")
        stats_done = sem("stats_done")
        std_done = sem("std_done")
        rstd_done = sem("rstd_done")
        ln_done = sem("ln_done")
        x1t_ready = sem("x1t_ready")
        x1t_hi = sem("x1t_hi")
        x1t_split = sem("x1t_split")
        below_done = sem("below_done")
        tern_done = sem("tern_done")
        up_ready = sem("up_ready")
        gate_ready = sem("gate_ready")
        down_ready = sem("down_ready")
        silu_done = sem("silu_done")
        hid_done = sem("hid_done")
        hid_hi = sem("hid_hi")
        hid_split = sem("hid_split")
        down_added = sem("down_added")
        stored = sem("stored")

        first = ([("k", 0, 0)] + [("x", 0, k) for k in range(KT)] + [("q", 0, 0), ("v", 0, 0)]
                 + [("q", 0, h) for h in (1, 2, 3)] + [("x", b, k) for b in (1, 2, 3) for k in range(KT)])
        current = [("d", 0, h) for h in range(HPG)]
        ahead = [("k", 1, 0), ("q", 1, 0), ("v", 1, 0), ("q", 1, 1), ("q", 1, 2), ("q", 1, 3)]
        PER_G = len(current) + len(ahead)
        assert PER_G % RAW == 0
        N_FIRST = len(first)
        slot_of = {}
        landed_at = {}
        for m, piece in enumerate(first):
            slot_of["first", piece] = m % RAW
            landed_at["first", piece] = 16 * (m // RAW + 1)
        for m, piece in enumerate(current + ahead):
            slot_of["loop", piece] = (N_FIRST + m) % RAW
            landed_at["loop", piece] = 16 * ((N_FIRST + m) // RAW + 1)
        PER_SLOT = 16 * (PER_G // RAW)
        on_vector = ([("x", 0, k) for k in range(KT)] + [("k", 0, 0), ("q", 0, 0), ("v", 0, 0), ("q", 0, 1)])
        on_vector.sort(key=first.index)
        on_pool_x = [p for p in first if p[0] == "x" and p not in on_vector]
        on_pool_w = [p for p in first if p[0] != "x" and p not in on_vector]
        NW_FIRST = len(on_pool_w)

        def parts(piece):
            kind, i, j = piece
            at = slice(i * S, (i + 1) * S)
            return {"x": lambda: (xt_hi[:, j, at], xt_lo[:, j, at]),
                    "k": lambda: (wk_hi[:], wk_lo[:]), "v": lambda: (wv_hi[:], wv_lo[:]),
                    "q": lambda: (wa_hi[:, j, :], wa_lo[:, j, :]),
                    "d": lambda: (wd_hi[:, j, :], wd_lo[:, j, :])}[kind]()

        def after(i, n):
            return nc.s_assert_within(i + 1, 1, n - 1,
                                      skip_runtime_bounds_check_because="under If(i < n - 1)")

        def source(piece, g):
            kind, ahead_by, j = piece
            if kind == "x":
                return x_t[ahead_by, j]
            at = after(g, G) if ahead_by else g
            return {"k": w_k, "v": w_v}[kind][at] if kind in "kv" else {"q": w_q, "d": w_dense}[kind][at, j]

        LANDED0 = 16 * (G * 3 * ET // FRAW)
        PER_C = 16 * (3 * ET // FRAW)

        START = 5

        block = ctx.enter_context(nc.Block())

        @block.sync
        def _(sp):
            def release(piece):
                if piece in on_vector:
                    sp.wait_ge(first_split, on_vector.index(piece) + 1)
                elif piece in on_pool_x:
                    sp.wait_ge(x_split_pool, on_pool_x.index(piece) + 1)
                else:
                    sp.wait_ge(w_split, on_pool_w.index(piece) + 1)

            for m, piece in enumerate(first):
                if m >= RAW:
                    release(first[m - RAW])
                sp.dma_start(raw[:, m % RAW, :], source(piece, 0)).then_inc(raw_landed[m % RAW], 16)
            for b in range(B):
                sp.dma_start(resid[:, b * QT:(b + 1) * QT, :], x_nat[b]).then_inc(resid_loaded, 16)

            for piece in first[-RAW:]:
                release(piece)
            with sp.Fori(0, G) as g:
                def load(m):
                    piece = (current + ahead)[m]
                    s = slot_of["loop", piece]
                    if m >= RAW:
                        sp.wait_ge(w_split, g * PER_G + NW_FIRST + m - RAW + 1)
                    sp.dma_start(raw[:, s, :], source(piece, g)).then_inc(raw_landed[s], 16)

                sp.wait_ge(w_split, g * PER_G + NW_FIRST)
                for m in range(len(current)):
                    load(m)
                with sp.If(g < G - 1):
                    for m in range(len(current), PER_G):
                        load(m)

            sp.wait_ge(abs_done, START + G * 3 * ET)
            order0 = [(w, et) for et in range(ET) for w in (0, 1)]
            for m, (w, et) in enumerate(order0):
                if m >= FRAW:
                    sp.wait_ge(tern_done, m - FRAW + 1)
                sp.dma_start(fraw[:, m % FRAW, :], (w_up, w_gate)[w][0, et]).then_inc(fraw_landed[m % FRAW], 16)
            with sp.Fori(0, C) as c:
                for m in range(3 * ET):
                    if m < ET:
                        sp.wait_ge(tern_done, c * 3 * ET + 2 * ET + m - FRAW + 1)
                        sp.dma_start(fraw[:, m % FRAW, :], w_down[c, m]).then_inc(fraw_landed[m % FRAW], 16)
                with sp.If(c < C - 1):
                    for m, (w, et) in enumerate(order0):
                        m += ET
                        sp.wait_ge(tern_done, c * 3 * ET + 2 * ET + m - FRAW + 1)
                        sp.dma_start(fraw[:, m % FRAW, :], (w_up, w_gate)[w][after(c, C), et]).then_inc(
                            fraw_landed[m % FRAW], 16)

            for b in range(B - 1):
                sp.wait_ge(ln_done, B * QT + (b + 1) * QT)
                sp.dma_start(out_nat[b], resid[:, b * QT:(b + 1) * QT, :]).then_inc(stored, 16)
            for t in range(QT):
                sp.wait_ge(ln_done, (2 * B - 1) * QT + t + 1)
                sp.dma_start(out_nat[B - 1][:, t, :], resid[:, (B - 1) * QT + t, :]).then_inc(stored, 16)
            sp.wait_ge(stored, 16 * (B - 1 + QT))

        @block.gpsimd
        def _(pool):
            nc.gpsimd.memset(ones[:], 1.0).then_inc(ones_set, 1)
            nc.gpsimd.memset(mask[:], 0.0).then_inc(zeroed, 1)
            nc.gpsimd.memset(ident[:], 0.0).then_inc(zeroed, 1)
            nc.gpsimd.memset(power[:], -0.5).then_inc(consts, 1)
            nc.gpsimd.memset(abs_tot[:], 0.0).then_inc(consts, 1)
            pool.wait_ge(zeroed, 2)
            nc.gpsimd.affine_select(out=mask[:, S - P:S], in_=mask[:, S - P:S], compare_op=ALU.is_ge, fill=NEG,
                                    base=0, pattern=[[-1, P]], channel_multiplier=1).then_inc(consts, 1)
            nc.gpsimd.affine_select(out=ident[:], in_=ident[:], compare_op=ALU.not_equal, fill=1.0,
                                    base=0, pattern=[[-1, P]], channel_multiplier=1).then_inc(consts, 1)

            def wait_apart():
                pool.sem_inc(pool_passed, 1)

            def round_to(dst, src):
                wide = ones[:, 0:P].unsqueeze(1).to_broadcast([P, 4, P])
                return nc.gpsimd.tensor_tensor(dst.rearrange("p (a b) -> p a b", b=P),
                                               src.rearrange("p (a b) -> p a b", b=P), wide, ALU.mult)

            pool.wait_ge(ones_set, 1)
            pool.sem_inc(wk_split, 1)
            pool.sem_inc(wv_split, 1)
            pool.sem_inc(wq_split, 2)

            def weight(piece, phase, base_landed, n_hi):
                s = slot_of[phase, piece]
                pool.wait_ge(raw_landed[s], base_landed + landed_at[phase, piece])
                hi, lo = parts(piece)
                done = {"k": wk_split, "v": wv_split, "q": wq_split, "d": wd_split}[piece[0]]
                wait_apart()
                round_to(hi, raw[:, s, :]).then_inc(w_hi_done, 1)
                pool.wait_ge(w_hi_done, n_hi)
                nc.gpsimd.tensor_tensor(lo, raw[:, s, :], hi.bitcast(F32), ALU.subtract).then_inc(w_split, 1)
                pool.wait_ge(w_split, n_hi)
                pool.sem_inc(done, 1)

            for m, piece in enumerate(on_pool_w):
                weight(piece, "first", 0, m + 1)
            for m, piece in enumerate(on_pool_x):
                s = slot_of["first", piece]
                pool.wait_ge(raw_landed[s], landed_at["first", piece])
                hi, lo = parts(piece)
                round_to(hi, raw[:, s, :]).then_inc(x_hi_pool, 1)
                pool.wait_ge(x_hi_pool, m + 1)
                nc.gpsimd.tensor_tensor(lo, raw[:, s, :], hi.bitcast(F32), ALU.subtract).then_inc(x_split_pool, 1)

            with pool.Fori(0, G) as g:
                for n in range(N):
                    if n in (2, 3):
                        pool.wait_ge(out_ready, START + g * N)
                        for m in (2 * (n - 2), 2 * (n - 2) + 1):
                            weight(current[m], "loop", g * PER_SLOT, g * PER_G + NW_FIRST + m + 1)
                    when = {12: (0, 1), 13: (2, 3), 14: (4,), 15: (5,)}
                    if n in when:
                        with pool.If(g < G - 1):
                            for m in when[n]:
                                kind, _, j = ahead[m]
                                if kind == "k":
                                    pool.wait_ge(k_ready, g * B + B)
                                elif kind == "v":
                                    pool.wait_ge(vt_ready, g * B + B)
                                else:
                                    pool.wait_ge(q_ready, g * N + N - HPG + j + 1)
                                weight(ahead[m], "loop", g * PER_SLOT, g * PER_G + NW_FIRST + 4 + m + 1)

            def one_over_std(at, tiles, before):
                pool.wait_ge(stats_done, tiles)
                nc.gpsimd.tensor_scalar(std[:, at], mv[:, at, 1], LN_EPS, None, ALU.add).then_inc(std_done, 1)
                pool.wait_ge(std_done, before + 1)
                nc.gpsimd.tensor_tensor(rstd[:, at], std[:, at], power[:, at], ALU.pow).then_inc(rstd_done, 1)

            def batch_one_over_std(batches):
                one_over_std(slice(0, QT), (batches + 1) * QT, batches)

            def compare_below(which, base, m, pieces):
                pool.wait_ge(fraw_landed[m % FRAW], base + LANDED0 + 16 * (m // FRAW + 1))
                if m >= len(below):
                    pool.wait_ge(tern_done, pieces - len(below) + 1)
                wait_apart()
                nc.gpsimd.tensor_scalar(below[m % len(below)], fraw[:, m % FRAW, :], nthr[:, which:which + 1], None,
                                        ALU.is_lt).then_inc(below_done, 1)

            batch_one_over_std(0)
            batch_one_over_std(1)
            pool.wait_ge(step, 4)
            for m in range(6):
                compare_below(m % 2, 0, m, m)
            batch_one_over_std(2)
            for m in (6, 7):
                compare_below(m % 2, 0, m, m)
            with pool.Fori(0, C) as c:
                for m in range(2 * ET, 3 * ET):
                    compare_below(2, c * PER_C, m, c * 3 * ET + m)
                with pool.If(c < 1):
                    batch_one_over_std(3)
                with pool.If(c < C - 1):
                    for m in range(3 * ET, 5 * ET):
                        compare_below(m % 2, c * PER_C, m, c * 3 * ET + m)
                with pool.If(c > C - 2):
                    for batches in range(B, 2 * B - 1):
                        batch_one_over_std(batches)
            for t in range(QT):
                one_over_std(slice(t, t + 1), (2 * B - 1) * QT + t + 1, 2 * B - 1 + t)

        @block.scalar
        def _(act):
            copy = nc.scalar.copy
            for s in (pt_hi_done, ctx_hi, abs_done):
                act.sem_inc(s, START)
            for m, piece in enumerate(on_vector):
                s = slot_of["first", piece]
                act.wait_ge(raw_landed[s], landed_at["first", piece])
                copy(parts(piece)[0], raw[:, s, :]).then_inc(first_hi, 1)
            act.wait_ge(k_ready, 1)
            copy(kt[:, 0, :], ps[:, OUT_BANK, :]).then_inc(k_hi, 1)
            act.wait_ge(q_ready, 1)
            copy(qt_hi[:], ps[:, Q_BANK, :]).then_inc(q_hi, 1)

            def pt_evacuate(head, chunk):
                _, at, w = PT_CHUNKS[chunk]
                act.wait_ge(pt_ready, START + head * 3 - 2 + chunk)
                copy(pt_hi[:, at:at + w], ps[:, PT_BANKS[chunk], 0:w]).then_inc(pt_hi_done, 1)

            def ctx_evacuate(head, b, h):
                act.wait_ge(ctx_ready, START + head)
                copy(mid_hi[:, b % 2, h, :], ps[:, CTX_BANK, :]).then_inc(ctx_hi, 1)

            def next_q(g, n):
                act.wait_ge(q_ready, g * N + n + 2)
                copy(qt_hi[:], ps[:, Q_BANK, :]).then_inc(q_hi, 1)

            def next_k(g, b):
                act.wait_ge(k_ready, g * B + b + 2)
                copy(kt[:, 0, :], ps[:, OUT_BANK, :]).then_inc(k_hi, 1)

            def load_ffn(at, n):
                which, et = divmod(n, ET)
                act.dma_start(fraw[:, n % FRAW, :], (w_up, w_gate, w_down)[which][at, et]).then_inc(
                    fraw_landed[n % FRAW], 16)

            for n in range(FRAW - 1):
                load_ffn(0, n)
            def x1_high(m):
                act.wait_ge(x1t_ready, m + 1)
                k, at, bank = x1_at(m)
                copy(xt_hi[:, k, at], ps[:, bank, :]).then_inc(x1t_hi, 1)

            def silu(c, u):
                act.wait_ge(up_ready, c * N + u + 1)
                if u >= 2:
                    act.wait_ge(hid_done, START + c * N + u - 1)
                nc.scalar.activation(sil[:, u % 2, :], ps[:, UP_BANKS[u % 2], :], ACT.Silu,
                                     scale=scales[:, 0:1]).then_inc(silu_done, 1)

            def hidden_high(c, u):
                b, et = divmod(u, ET)
                act.wait_ge(hid_done, START + c * N + u + 1)
                copy(mid_hi[:, b % 2, et, :], hid[u % 2]).then_inc(hid_hi, 1)

            with act.Fori(0, G) as g:
                for n in range(N):
                    b, h = divmod(n, HPG)
                    before = (b, h - 1) if h else ((b - 1) % B, HPG - 1)
                    if n:
                        pt_evacuate(g * N + n, 0)
                        pt_evacuate(g * N + n, 1)
                    else:
                        with act.If(g > 0):
                            pt_evacuate(g * N + n, 0)
                            pt_evacuate(g * N + n, 1)
                    if n:
                        pt_evacuate(g * N + n, 2)
                    else:
                        with act.If(g > 0):
                            pt_evacuate(g * N + n, 2)
                    if n in early_x1:
                        with act.If(g > G - 2):
                            x1_high(early_x1[n])
                    act.wait_ge(negmax_done, g * N + n + 1)
                    for i in TILE_ORDER:
                        t = probs[:, n % 2, S_SBUF[i]:S_SBUF[i] + P * (i + 1)]
                        nc.scalar.activation(t, t, ACT.Exp, bias=negmax[:, n % 2, i:i + 1], scale=SCALE,
                                             accum_out=rowsum[:, n % 2, i:i + 1]).then_inc(exp_done, 1)
                    if n < N - 1:
                        next_q(g, n)
                    else:
                        with act.If(g < G - 1):
                            next_q(g, n)
                    if n < 3 * ET:
                        which, et = divmod(n, ET)
                        s = n % FRAW
                        act.wait_ge(fraw_landed[s], g * 16 * (3 * ET // FRAW) + 16 * (n // FRAW + 1))
                        act.wait_ge(abs_added, START + g)
                        nc.scalar.activation(fraw[:, s, :], fraw[:, s, :], ACT.Abs,
                                             accum_out=abs_part[:, which, et:et + 1]).then_inc(abs_done, 1)
                        if n + FRAW - 1 < 3 * ET:
                            act.wait_ge(abs_done, START + g * 3 * ET + n)
                            load_ffn(g, n + FRAW - 1)
                        else:
                            with act.If(g < G - 1):
                                act.wait_ge(abs_done, START + g * 3 * ET + n)
                                load_ffn(after(g, G), n + FRAW - 1 - 3 * ET)
                    if h == 3:
                        if b < B - 1:
                            next_k(g, b)
                        else:
                            with act.If(g < G - 1):
                                next_k(g, b)
                    if h == 0:
                        act.wait_ge(vt_ready, g * B + b + 1)
                        copy(vt[:], ps[:, OUT_BANK, :]).then_inc(vt_copied, 1)
                    if n:
                        ctx_evacuate(g * N + n, *before)
                    else:
                        with act.If(g > 0):
                            ctx_evacuate(g * N + n, *before)
                    if h == 0:
                        act.wait_ge(v_ready, g * B + b + 1)
                        copy(v_hi[:], ps[:, OUT_BANK, :]).then_inc(v_hi_done, 1)

            pt_evacuate(G * N, 0)
            pt_evacuate(G * N, 1)
            pt_evacuate(G * N, 2)
            silu(0, 0)
            hidden_high(0, 0)
            silu(0, 1)
            hidden_high(0, 1)
            ctx_evacuate(G * N, B - 1, HPG - 1)
            silu(0, 2)
            hidden_high(0, 2)
            for m in range(N_EARLY, 2 * KT):
                x1_high(m)
            silu(0, 3)
            hidden_high(0, 3)
            with act.Fori(0, C) as c:
                for u in range(N):
                    b, et = divmod(u, ET)
                    if b:
                        silu(c, u)
                        hidden_high(c, u)
                    else:
                        with act.If(c > 0):
                            silu(c, u)
                            hidden_high(c, u)
                    if u in late_x1:
                        with act.If(c < 1):
                            for m in late_x1[u]:
                                x1_high(m)

        @block.vector
        def _(dve):
            for s in (pt_split, ctx_split, out_added, down_added, masked, normed, v_split, abs_added, hid_done,
                      hid_split):
                dve.sem_inc(s, START)
            links = [0]

            def link(ins):
                links[0] += 1
                ins.then_inc(step, 1)
                dve.wait_ge(step, links[0])

            def low(lo, src, hi):
                return nc.vector.tensor_tensor(lo, src, hi.bitcast(F32), ALU.subtract)

            for m, piece in enumerate(on_vector):
                hi, lo = parts(piece)
                dve.wait_ge(first_hi, m + 1)
                low(lo, raw[:, slot_of["first", piece], :], hi).then_inc(first_split, 1)
            dve.wait_ge(k_hi, 1)
            low(kt[:, 1, :], ps[:, OUT_BANK, :], kt[:, 0, :]).then_inc(k_split, 1)
            dve.wait_ge(q_hi, 1)
            low(qt_lo[:], ps[:, Q_BANK, :], qt_hi[:]).then_inc(q_split, 1)
            dve.wait_ge(consts, 4)

            def pt_low(head, chunk):
                _, at, w = PT_CHUNKS[chunk]
                dve.wait_ge(pt_hi_done, START + head * 3 - 2 + chunk)
                low(pt_lo[:, at:at + w], ps[:, PT_BANKS[chunk], 0:w], pt_hi[:, at:at + w]).then_inc(pt_split, 1)

            def ctx_low(head, b, h):
                dve.wait_ge(ctx_hi, START + head)
                low(mid_lo[:, b % 2, h, :], ps[:, CTX_BANK, :], mid_hi[:, b % 2, h, :]).then_inc(ctx_split, 1)

            def next_q(g, n):
                dve.wait_ge(q_hi, g * N + n + 2)
                low(qt_lo[:], ps[:, Q_BANK, :], qt_hi[:]).then_inc(q_split, 1)

            def next_k(g, b):
                dve.wait_ge(k_hi, g * B + b + 2)
                low(kt[:, 1, :], ps[:, OUT_BANK, :], kt[:, 0, :]).then_inc(k_split, 1)

            def add_out(tiles, b, t, bank=OUT_BANK):
                dve.wait_ge(out_ready, START + tiles)
                dve.wait_ge(resid_loaded, 16 * B)
                r = resid[:, b * QT + t, :]
                nc.vector.tensor_tensor(r, ps[:, bank, :], r, ALU.add).then_inc(out_added, 1)

            def take_stats(b, t):
                nc.vector.bn_stats(stats[:, t, :], resid[:, b * QT + t, :]).then_inc(bn_done, 1)

            def aggregate(t, tiles):
                dve.wait_ge(bn_done, tiles)
                nc.vector.bn_aggr(mv[:, t, :], stats[:, t, :]).then_inc(stats_done, 1)

            def batch_stats(b, tiles=range(QT)):
                for t in tiles:
                    take_stats(b, t)

            def batch_aggregate(batches):
                if batches:
                    dve.wait_ge(ln_done, batches * QT)
                for t in range(QT):
                    aggregate(t, (batches + 1) * QT)

            def normalise(b, t):
                r = resid[:, b * QT + t, :]
                nc.vector.tensor_scalar(r, r, mv[:, t, 0:1], rstd[:, t:t + 1], ALU.subtract,
                                        ALU.mult).then_inc(ln_done, 1)

            def batch_normalise(b, batches):
                dve.wait_ge(rstd_done, batches + 1)
                for t in range(QT):
                    normalise(b, t)

            def x1_low(m):
                dve.wait_ge(x1t_hi, m + 1)
                k, at, bank = x1_at(m)
                low(xt_lo[:, k, at], ps[:, bank, :], xt_hi[:, k, at]).then_inc(x1t_split, 1)

            def ternary(which, et, m, pieces):
                dve.wait_ge(below_done, pieces + 1)
                nc.vector.scalar_tensor_tensor((wa_hi, wa_lo, wd_hi)[which][:, et, :], fraw[:, m % FRAW, :],
                                               thr[:, which:which + 1], below[m % len(below)], ALU.is_gt,
                                               ALU.subtract).then_inc(tern_done, 1)

            def first_ternary(m):
                et, w = divmod(m, 2)
                dve.wait_ge(q_ready, (G - 1) * N + N - HPG + et + 1)
                ternary(w, et, m, m)

            def ffn_scales():
                dve.wait_ge(tot_ready, 1)
                link(nc.vector.tensor_scalar(scales[:, 0:3], TOT, 1.0 / (D * E), QUANT_EPS, ALU.mult, ALU.add))
                link(nc.vector.tensor_scalar(thr[:, 0:3], scales[:, 0:3], 0.5, None, ALU.mult))
                link(nc.vector.tensor_scalar(nthr[:, 0:3], scales[:, 0:3], -0.5, None, ALU.mult))
                link(nc.vector.tensor_tensor(scales[:, 3:4], scales[:, 1:2], scales[:, 2:3], ALU.mult))

            def early_ffn(n):
                if n in early_x1:
                    x1_low(early_x1[n])
                if n in (7, 11):
                    batch_stats((n - 7) // 4)
                if n in (8, 12):
                    batch_normalise((n - 8) // 4, (n - 8) // 4)
                if n == 12:
                    dve.wait_ge(abs_added, START + G)
                    nc.vector.tensor_reduce(abs_sum[:, 0:3], abs_tot[:], mybir.AxisListType.X,
                                            ALU.add).then_inc(tot_done, 1)
                if n == 13:
                    ffn_scales()
                if n == 14:
                    first_ternary(0)
                    first_ternary(1)
                if n == 15:
                    batch_stats(2, (0, 1, 2))

            def hidden(c, u):
                dve.wait_ge(silu_done, c * N + u + 1)
                dve.wait_ge(gate_ready, c * N + u + 1)
                if u >= 2:
                    dve.wait_ge(hid_split, START + c * N + u - 1)
                nc.vector.tensor_tensor(hid[u % 2], ps[:, GATE_BANKS[u % 2], :], sil[:, u % 2, :],
                                        ALU.mult).then_inc(hid_done, 1)

            def hidden_low(c, u):
                b, et = divmod(u, ET)
                dve.wait_ge(hid_hi, c * N + u + 1)
                low(mid_lo[:, b % 2, et, :], hid[u % 2], mid_hi[:, b % 2, et, :]).then_inc(hid_split, 1)

            with dve.Fori(0, G) as g:
                for n in range(N):
                    b, h = divmod(n, HPG)
                    before = (b, h - 1) if h else ((b - 1) % B, HPG - 1)
                    if n:
                        pt_low(g * N + n, 0)
                        pt_low(g * N + n, 1)
                    else:
                        with dve.If(g > 0):
                            pt_low(g * N + n, 0)
                            pt_low(g * N + n, 1)
                    dve.wait_ge(scores_ready, (g * N + n) * 3 + 1)
                    first = probs[:, n % 2, S_SBUF[0]:S_SBUF[0] + P]
                    nc.vector.tensor_tensor(first, flat[:, S_PSUM[0] + P:S_PSUM[0] + 2 * P], mask[:, S - P:S],
                                            ALU.add).then_inc(tile0_masked, 1)
                    for i in (1, 0, 2, 3):
                        w = P * (i + 1)
                        if i != 1:
                            if i:
                                dve.wait_ge(scores_ready, (g * N + n) * 3 + i)
                            else:
                                dve.wait_ge(tile0_masked, g * N + n + 1)
                            dve.sem_inc(dve_passed, 1)
                        nc.vector.tensor_tensor_reduce(
                            out=probs[:, n % 2, S_SBUF[i]:S_SBUF[i] + w], in0=flat[:, S_PSUM[i]:S_PSUM[i] + w],
                            in1=mask[:, S - w:S] if i else first, scale=1.0, scalar=NEG, op0=ALU.add, op1=ALU.max,
                            accum_out=rowmax[:, n % 2, i:i + 1]).then_inc(masked, 1)
                    dve.wait_ge(masked, START + (g * N + n) * 4 + 4)
                    nc.vector.tensor_scalar(negmax[:, n % 2, :], rowmax[:, n % 2, :], -SCALE, None,
                                            ALU.mult).then_inc(negmax_done, 1)
                    if n:
                        pt_low(g * N + n, 2)
                    else:
                        with dve.If(g > 0):
                            pt_low(g * N + n, 2)
                    tiles = {1: (0, 1), 2: (2, 3)}.get(h)
                    if tiles:
                        if b:
                            add_out(g * N + (b - 1) * QT + tiles[0] + 1, b - 1, tiles[0])
                        else:
                            with dve.If(g > 0):
                                add_out(g * N - QT + tiles[0] + 1, B - 1, tiles[0])
                    if n == 3 * ET:
                        dve.wait_ge(abs_done, START + (g + 1) * 3 * ET)
                        dve.wait_ge(abs_added, START + g)
                        nc.vector.tensor_tensor(abs_tot[:], abs_tot[:], abs_part[:], ALU.add).then_inc(abs_added, 1)
                    if n >= 7:
                        with dve.If(g > G - 2):
                            early_ffn(n)
                    if n < N - 1:
                        next_q(g, n)
                    else:
                        with dve.If(g < G - 1):
                            next_q(g, n)
                    dve.wait_ge(exp_done, (g * N + n) * 4 + 4)
                    nc.vector.reciprocal(rinv[:, n % 2, :], rowsum[:, n % 2, :]).then_inc(rinv_done, 1)
                    dve.wait_ge(rinv_done, g * N + n + 1)
                    for i in TILE_ORDER:
                        t = probs[:, n % 2, S_SBUF[i]:S_SBUF[i] + P * (i + 1)]
                        nc.vector.tensor_scalar(t, t, rinv[:, n % 2, i:i + 1], None, ALU.mult).then_inc(normed, 1)
                    if tiles:
                        if b:
                            add_out(g * N + (b - 1) * QT + tiles[1] + 1, b - 1, tiles[1])
                        else:
                            with dve.If(g > 0):
                                add_out(g * N - QT + tiles[1] + 1, B - 1, tiles[1])
                    if n == N - 2:
                        with dve.If(g > G - 2):
                            first_ternary(2)
                            first_ternary(3)
                    if h == 3:
                        if b < B - 1:
                            next_k(g, b)
                        else:
                            with dve.If(g < G - 1):
                                next_k(g, b)
                    if n:
                        ctx_low(g * N + n, *before)
                    else:
                        with dve.If(g > 0):
                            ctx_low(g * N + n, *before)
                    if n in (7, 11):
                        with dve.If(g > G - 2):
                            batch_aggregate((n - 7) // 4)
                    if h == 0:
                        dve.wait_ge(v_hi_done, g * B + b + 1)
                        low(v_lo[:], ps[:, OUT_BANK, :], v_hi[:]).then_inc(v_split, 1)

            def add_down(tiles, b, t, bank):
                dve.wait_ge(down_ready, START + tiles)
                r = resid[:, b * QT + t, :]
                nc.vector.scalar_tensor_tensor(r, ps[:, bank, :], scales[:, 3:4], r,
                                               ALU.mult, ALU.add).then_inc(down_added, 1)

            pt_low(G * N, 0)
            pt_low(G * N, 1)
            batch_stats(2, (3,))
            batch_aggregate(2)
            pt_low(G * N, 2)
            first_ternary(4)
            first_ternary(5)
            hidden(0, 0)
            hidden_low(0, 0)
            hidden(0, 1)
            hidden_low(0, 1)
            ctx_low(G * N, B - 1, HPG - 1)
            batch_normalise(2, 2)
            first_ternary(6)
            first_ternary(7)
            hidden(0, 2)
            hidden_low(0, 2)
            add_out(G * N - 3, B - 1, 0, DOWN_BANKS[0])
            for m in range(N_EARLY, 2 * KT):
                x1_low(m)
            add_out(G * N - 2, B - 1, 1, DOWN_BANKS[1])
            add_out(G * N - 1, B - 1, 2, DOWN_BANKS[0])
            hidden(0, 3)
            hidden_low(0, 3)
            add_out(G * N, B - 1, 3, DOWN_BANKS[1])

            with dve.Fori(0, C) as c:
                for u in range(N):
                    b, et = divmod(u, ET)

                    if u in (3, 4):
                        turn = [(2, e, 2 * ET + e) for e in ((0, 1) if u == 3 else (2, 3))]
                    elif b == B - 1:
                        turn = [(w, et, 3 * ET + 2 * et + w) for w in (0, 1)]
                    else:
                        turn = None

                    def next_ternary(a):
                        which, e, m = turn[a]
                        if which == 2:
                            dve.wait_ge(down_ready, START + c * N)
                            ternary(which, e, m, c * 3 * ET + m)
                        else:
                            with dve.If(c < C - 1):
                                ternary(which, e, m, c * 3 * ET + m)

                    def slot():
                        hidden(c, u)
                        for t in {1: (0, 1), 2: (2, 3)}.get(et, ()):
                            add_down(c * N + (b - 1) * QT + t + 1, (b - 1) % B, t, DOWN_BANKS[t % 2])

                    if b:
                        slot()
                    else:
                        with dve.If(c > 0):
                            slot()
                    if turn:
                        next_ternary(0)
                    if et == 3 and b:
                        with dve.If(c > C - 2):
                            dve.wait_ge(rstd_done, B + b)
                            normalise(b - 1, 0)
                            normalise(b - 1, 1)
                    if b:
                        hidden_low(c, u)
                    else:
                        with dve.If(c > 0):
                            hidden_low(c, u)
                    if turn:
                        next_ternary(1)
                    if et and b:
                        with dve.If(c > C - 2):
                            if et == 3:
                                normalise(b - 1, 2)
                                normalise(b - 1, 3)
                            else:
                                dve.wait_ge(down_added, START + (C - 1) * N + (b - 1) * QT + 2 * et)
                                batch_stats(b - 1, (2 * et - 2, 2 * et - 1))
                                if et == 2:
                                    batch_aggregate(B + b - 1)
                    if u in late_x1:
                        with dve.If(c < 1):
                            for m in late_x1[u]:
                                x1_low(m)
                    if u in (ET + 2, ET + 3, ET + 4):
                        with dve.If(c < 1):
                            if u == ET + 2:
                                batch_stats(3)
                                batch_aggregate(3)
                            else:
                                dve.wait_ge(rstd_done, 4)
                                for t in (0, 1) if u == ET + 3 else (2, 3):
                                    normalise(3, t)
            done = (2 * B - 1) * QT

            def last_normalise(t):
                dve.wait_ge(rstd_done, 2 * B + t)
                normalise(B - 1, t)

            for t in range(QT):
                add_down(C * N - QT + t + 1, B - 1, t, DOWN_BANKS[t])
                dve.wait_ge(down_added, START + C * N - QT + t + 1)
                take_stats(B - 1, t)
                if t == 0:
                    dve.wait_ge(ln_done, done)
                aggregate(t, done + t + 1)
                if t == 1:
                    last_normalise(0)
            for t in (1, 2, 3):
                last_normalise(t)

        @block.tensor
        def _(pe):
            mm = nc.tensor.matmul
            for s in (pt_ready, out_ready, down_ready, ctx_ready):
                pe.sem_inc(s, START)

            def product(bank_ap, terms):
                for n, (w, v) in enumerate(terms):
                    last = mm(bank_ap, w, v, start=n == 0, stop=n == len(terms) - 1)
                return last

            def project(bank, w_hi, w_lo, b):
                at = slice(b * S, (b + 1) * S)
                return product(ps[:, bank, :], [
                    t for k in range(KT) for t in (
                        (w_hi[:, k * P:(k + 1) * P], xt_hi[:, k, at]),
                        (w_hi[:, k * P:(k + 1) * P], xt_lo[:, k, at]),
                        (w_lo[:, k * P:(k + 1) * P], xt_hi[:, k, at]))])

            def x_of(b):
                pe.wait_ge(x_split_pool, b * KT)

            def q_project(b, h):
                project(Q_BANK, wa_hi[:, h, :], wa_lo[:, h, :], b).then_inc(q_ready, 1)

            def k_project(b):
                project(OUT_BANK, wk_hi[:], wk_lo[:], b).then_inc(k_ready, 1)

            def transpose_chunk(par, chunk):
                js, _, _ = PT_CHUNKS[chunk]
                at = 0
                for j in js:
                    for i in range(j, QT):
                        last = nc.tensor.transpose(ps[:, PT_BANKS[chunk], at:at + P],
                                                   probs[:, par, S_SBUF[i] + j * P:S_SBUF[i] + (j + 1) * P], ident[:])
                        at += P
                last.then_inc(pt_ready, 1)

            def transposes_ab(heads, par):
                pe.wait_ge(normed, START + heads * 4 + 4)
                pe.wait_ge(pt_split, START + heads * 3)
                transpose_chunk(par, 0)
                transpose_chunk(par, 1)

            def transposes_c(heads, par):
                pe.wait_ge(pt_split, START + heads * 3 + 1)
                transpose_chunk(par, 2)

            def pv(heads, batches):
                pe.wait_ge(pt_split, START + heads * 3 + 3)
                pe.wait_ge(v_split, START + batches)
                pe.wait_ge(ctx_split, START + heads)
                n = 0
                for j in (0, 1, 3, 2):
                    w = S - j * P
                    at = PT_AT[j]
                    for v, p in ((v_hi, pt_hi), (v_hi, pt_lo), (v_lo, pt_hi)):
                        last = mm(ps[:, CTX_BANK, j * P:S], v[:, j * P:(j + 1) * P], p[:, at:at + w],
                                  start=n == 0, stop=n == 3 * QT - 1)
                        n += 1
                last.then_inc(ctx_ready, 1)

            def out_tile(tiles, par, t, bank=OUT_BANK, in_turns=0):
                pe.wait_ge(out_added, START + tiles - in_turns)
                at = slice(t * P, (t + 1) * P)
                product(ps[:, bank, :], [
                    t for h in range(HPG) for t in (
                        (mid_hi[:, par, h, at], wd_hi[:, h, :]),
                        (mid_hi[:, par, h, at], wd_lo[:, h, :]),
                        (mid_lo[:, par, h, at], wd_hi[:, h, :]))]).then_inc(out_ready, 1)

            pe.wait_ge(ones_set, 1)
            for _ in range(WARM_UP):
                mm(ps[:, Q_BANK, 0:P], ones[:], ones[:], start=True, stop=True)

            need = {p: n + 1 for n, p in enumerate(on_vector)}
            for k in range(KT):
                pe.wait_ge(first_split, need["x", 0, k])
                at = slice(k * P, (k + 1) * P)
                for n, (w, v) in enumerate(((wk_hi, xt_hi), (wk_hi, xt_lo), (wk_lo, xt_hi))):
                    last = mm(ps[:, OUT_BANK, :], w[:, at], v[:, k, 0:S], start=k + n == 0,
                              stop=k == KT - 1 and n == 2)
            last.then_inc(k_ready, 1)
            pe.wait_ge(first_split, need["q", 0, 0])
            q_project(0, 0)
            pe.wait_ge(first_split, len(on_vector))
            pe.wait_ge(consts, 4)

            def x1_transpose(m):
                k, _, bank = x1_at(m)
                b = x1_tiles[m][0]
                pe.wait_ge(ln_done, (b + 1) * QT)
                if m >= N_EARLY + 2:
                    pe.wait_ge(x1t_split, m - 1)
                for t in range(QT):
                    last = nc.tensor.transpose(ps[:, bank, t * P:(t + 1) * P],
                                               resid[:, b * QT + t, k * P:(k + 1) * P], ident[:])
                last.then_inc(x1t_ready, 1)

            def half(bank, w, b):
                at = slice(b * S, (b + 1) * S)
                return product(ps[:, bank, :], [
                    (w[:, k * P:(k + 1) * P], v[:, k, at]) for k in range(KT) for v in (xt_hi, xt_lo)])

            def up(u):
                b, et = divmod(u, ET)
                half(UP_BANKS[u % 2], wa_hi[:, et, :], b).then_inc(up_ready, 1)

            def gate(u):
                b, et = divmod(u, ET)
                half(GATE_BANKS[u % 2], wa_lo[:, et, :], b).then_inc(gate_ready, 1)

            with pe.Fori(0, G) as g:
                for n in range(N):
                    b, h = divmod(n, HPG)
                    if n:
                        transposes_ab(g * N + n - 1, (n - 1) % 2)
                    else:
                        with pe.If(g > 0):
                            transposes_ab(g * N + n - 1, (n - 1) % 2)

                    pe.wait_ge(q_split, g * N + n + 1)
                    if h == 0:
                        pe.wait_ge(k_split, g * B + b + 1)
                    pe.wait_ge(masked, START + (g * N + n) * 4)
                    for i in TILE_ORDER:
                        at, w = slice(i * P, (i + 1) * P), P * (i + 1)
                        to = flat[:, S_PSUM[i]:S_PSUM[i] + w]
                        if i == 0:
                            mm(flat[:, S_PSUM[0]:S_PSUM[0] + 2 * P].rearrange("p (a s) -> p a s", a=2), qt_hi[:, at],
                               kt[:, :, 0:P], start=True, stop=False)
                            mm(to, qt_lo[:, at], kt[:, 0, 0:P], start=False, stop=True)
                            continue
                        last = product(to, [(qt_hi[:, at], kt[:, 0, 0:w]), (qt_hi[:, at], kt[:, 1, 0:w]),
                                            (qt_lo[:, at], kt[:, 0, 0:w])])
                        last.then_inc(scores_ready, 1)

                    if n:
                        transposes_c(g * N + n - 1, (n - 1) % 2)
                    else:
                        with pe.If(g > 0):
                            transposes_c(g * N + n - 1, (n - 1) % 2)
                    if n in early_x1:
                        with pe.If(g > G - 2):
                            pe.wait_ge(ctx_split, START + (G - 1) * N + n - 1)
                            x1_transpose(early_x1[n])
                    if n == 3 * ET + 1:
                        with pe.If(g > G - 2):
                            pe.wait_ge(tot_done, 1)
                            pe.wait_ge(ctx_split, START + (G - 1) * N + n - 1)
                            mm(TOT, ones[:], abs_sum[:, 0:3], start=True, stop=True).then_inc(tot_ready, 1)

                    tiles = {1: (0, 1), 2: (2, 3)}.get(h)

                    def out_of_batch_before(t, first):
                        if b:
                            if first:
                                pe.wait_ge(ctx_split, START + g * N + b * HPG)
                                pe.wait_ge(v_split, START + g * B + b + 1)
                                if b == 1:
                                    pe.wait_ge(wd_split, (g + 1) * HPG)
                            out_tile(g * N + (b - 1) * QT + t, (b - 1) % 2, t)
                        else:
                            with pe.If(g > 0):
                                if first:
                                    pe.wait_ge(ctx_split, START + g * N)
                                    pe.wait_ge(v_split, START + g * B + b + 1)
                                out_tile(g * N - QT + t, (B - 1) % 2, t)

                    if tiles:
                        out_of_batch_before(tiles[0], h == 1)

                    def next_q():
                        nb, nh = divmod((n + 1) % N, HPG)
                        if nh == 0:
                            x_of(nb)
                        if nb == 0:
                            pe.wait_ge(wq_split, (g + (1 if n == N - 1 else 0)) * HPG + nh + 1)
                        q_project(nb, nh)
                    if n < N - 1:
                        next_q()
                    else:
                        with pe.If(g < G - 1):
                            next_q()
                        with pe.If(g > G - 2):
                            pe.wait_ge(x1t_split, KT)
                            pe.wait_ge(tern_done, 2)
                            pe.wait_ge(out_added, START + (G - 1) * N + (B - 1) * QT)
                            up(0)
                            gate(0)

                    if tiles:
                        out_of_batch_before(tiles[1], False)
                    if h == 3:
                        if b < B - 1:
                            pe.wait_ge(out_added, START + g * N + b * QT)
                            k_project(b + 1)
                        else:
                            with pe.If(g < G - 1):
                                pe.wait_ge(out_added, START + g * N + b * QT)
                                pe.wait_ge(wk_split, g + 2)
                                k_project(0)
                    if h == 0:
                        if b == 0:
                            pe.wait_ge(wv_split, g + 1)
                        project(OUT_BANK, wv_hi[:], wv_lo[:], b).then_inc(vt_ready, 1)

                    if n in early_x1 or n == 3 * ET + 1:
                        with pe.If(g > G - 2):
                            if n in early_x1:
                                pe.wait_ge(x1t_split, early_x1[n] + 1)
                            else:
                                pe.wait_ge(step, 1)

                    def pv_before():
                        pv(g * N + n - 1, g * B + (b if h else b - 1) + 1)
                    if n:
                        pv_before()
                    else:
                        with pe.If(g > 0):
                            pv(g * N - 1, g * B)
                    if h == 0:
                        pe.wait_ge(vt_copied, g * B + b + 1)
                        for t in range(QT):
                            last = nc.tensor.transpose(ps[:, OUT_BANK, t * P:(t + 1) * P],
                                                       vt[:, t * P:(t + 1) * P], ident[:])
                        last.then_inc(v_ready, 1)

            transposes_ab(G * N - 1, (N - 1) % 2)
            pe.wait_ge(tern_done, 4)
            pe.wait_ge(masked, START + G * N * 4)
            up(1)
            transposes_c(G * N - 1, (N - 1) % 2)
            gate(1)
            pv(G * N - 1, G * B)
            pe.wait_ge(tern_done, 6)
            pe.wait_ge(hid_done, START + 1)
            up(2)
            gate(2)
            pe.wait_ge(ctx_split, START + G * N)
            out_tile(G * N - 4, (B - 1) % 2, 0, DOWN_BANKS[0], in_turns=0)
            for m in range(N_EARLY, 2 * KT):
                x1_transpose(m)
            pe.wait_ge(tern_done, 8)
            pe.wait_ge(hid_done, START + 2)
            up(3)
            out_tile(G * N - 3, (B - 1) % 2, 1, DOWN_BANKS[1], in_turns=1)
            gate(3)
            out_tile(G * N - 2, (B - 1) % 2, 2, DOWN_BANKS[0], in_turns=1)
            out_tile(G * N - 1, (B - 1) % 2, 3, DOWN_BANKS[1], in_turns=1)

            def down(bank, par, t, ets=range(ET)):
                at = slice(t * P, (t + 1) * P)
                for et in ets:
                    for v in (mid_hi, mid_lo):
                        last = mm(ps[:, bank, :], v[:, par, et, at], wd_hi[:, et, :],
                                  start=et == 0 and v is mid_hi, stop=et == ET - 1 and v is mid_lo)
                return last

            def down_tile(tiles, par, t):
                pe.wait_ge(down_added, START + tiles - (t if t < 2 else 1))
                down(DOWN_BANKS[t % 2], par, t).then_inc(down_ready, 1)

            with pe.Fori(0, C) as c:
                for u in range(N):
                    b, et = divmod(u, ET)

                    def slot():
                        if et == 0:
                            pe.wait_ge(x1t_split, (b + 1) * KT)
                        pe.wait_ge(hid_done, START + c * N + u - 1)
                        if b == 0:
                            pe.wait_ge(tern_done, c * 3 * ET + 2 * et + 2)
                        up(u)
                        gate(u)
                        for t in {1: (0, 1), 2: (2, 3)}.get(et, ()):
                            if t == 0:
                                pe.wait_ge(hid_split, START + c * N + b * ET)
                                if b == 1:
                                    pe.wait_ge(tern_done, (c + 1) * 3 * ET)
                                    pe.wait_ge(out_added, START + G * N)
                            down_tile(c * N + (b - 1) * QT + t, (b - 1) % 2, t)
                    if b:
                        slot()
                    else:
                        with pe.If(c > 0):
                            slot()
                    if u in late_x1:
                        with pe.If(c < 1):
                            for m in late_x1[u]:
                                x1_transpose(m)
            pe.wait_ge(down_added, START + C * N - QT)
            par = (B - 1) % 2
            pe.wait_ge(hid_split, START + C * N - 1)
            for t in (0, 1):
                down(DOWN_BANKS[t], par, t, (0, 1, 2))
            pe.wait_ge(hid_split, START + C * N)
            for t in range(QT):
                down(DOWN_BANKS[t], par, t, (3,) if t < 2 else range(ET)).then_inc(down_ready, 1)


def kernel(**inputs):
    import numpy as np
    import concourse.bacc as bacc
    from concourse.bass_utils import run_bass_kernel_spmd as run

    x = np.ascontiguousarray(inputs["L0_attn_x"])
    w_kv = inputs["L0_attn_w_kv"]

    def by_column(w, n):
        return np.ascontiguousarray(np.asarray(w).reshape(KT, P, n, P).transpose(2, 1, 0, 3).reshape(n, P, KT * P))

    arrays = {
        "x": x,
        "x_t": np.ascontiguousarray(np.asarray(x).transpose(0, 2, 1).reshape(B, KT, P, S)),
        "w_q": by_column(inputs["L0_attn_w_q"], G * HPG).reshape(G, HPG, P, KT * P),
        "w_k": by_column(w_kv[:, :G * DH], G),
        "w_v": by_column(w_kv[:, G * DH:], G),
        "w_dense": np.ascontiguousarray(inputs["L0_attn_w_dense"]).reshape(G, HPG, P, D),
        "w_up": by_column(np.asarray(inputs["L0_ffn_W_up"]).T, C * ET).reshape(C, ET, P, KT * P),
        "w_gate": by_column(np.asarray(inputs["L0_ffn_W_gate"]).T, C * ET).reshape(C, ET, P, KT * P),
        "w_down": np.ascontiguousarray(np.asarray(inputs["L0_ffn_W_down"]).T).reshape(C, ET, P, D),
    }
    nc = bacc.Bacc("TRN2", target_bir_lowering=False, num_devices=1, dynamic_dma_scratch_size=1024)
    args = [nc.dram_tensor(f"in_{name}", a.shape, mybir.dt.from_np(a.dtype), kind="ExternalInput").ap()
            for name, a in arrays.items()]
    args.append(nc.dram_tensor("out", (B, S, D), F32, kind="ExternalOutput").ap())
    layer(nc, *args)
    r = run(nc, [{f"in_{name}": a for name, a in arrays.items()}], core_ids=[0])
    return r.results[0]["out"]
```
